# Optimizing a Trainium2 kernel written in Bass

```python
import numpy as np
import jax
import jax.numpy as jnp

def _softmax(x, axis=-1):
    return jax.nn.softmax(x, axis=axis)

def _gelu(x):
    return jax.nn.gelu(x, approximate=True)

def _silu(x):
    return jax.nn.silu(x)

def _sigmoid(x):
    return jax.nn.sigmoid(x)

def _layernorm(x, axis=-1, eps=1e-05):
    m = jnp.mean(x, axis=axis, keepdims=True)
    v = jnp.var(x, axis=axis, keepdims=True)
    return (x - m) / jnp.sqrt(v + eps)

def _scatter_add(tgt, idx, src, axis=0):
    return tgt.at[idx].add(src)

def _segment_sum(src, seg, n):
    return jax.ops.segment_sum(src, seg, n)
kernel_name = 'mk_gnn_resnorm_d4_gnn_r8_13d711'

def setup_inputs(seed: int=0):
    np.random.seed(seed)
    _w = jnp.asarray

    def _rec_inputs():
        import jax
        import jax.numpy as jnp
        _gk = jax.random.key(seed)
        x = -0.0003713 + 1 * jax.random.normal(jax.random.fold_in(_gk, 1), (6250, 256), jnp.float32)
        _s = jax.random.randint(jax.random.fold_in(_gk, 2), (50000,), 0, 6250, jnp.int32)
        _d = jax.random.randint(jax.random.fold_in(_gk, 3), (50000,), 0, 6250, jnp.int32)
        _loop = jnp.arange(6250, dtype=jnp.int32)
        src = jnp.concatenate([_s, _d, _loop])
        dst = jnp.concatenate([_d, _s, _loop])
        _o = jnp.argsort(dst, stable=True)
        src = src[_o]
        dst = dst[_o]
        edge_weight = jax.random.uniform(jax.random.fold_in(_gk, 13), (106250,), jnp.float32, 0.0, 0.999998)
        return (x, src, dst, edge_weight)
    x, src, dst, edge_weight = _rec_inputs()

    def _L0_gnn_setup():
        import jax, jax.numpy as jnp
        import numpy as np
        N_NODES = 6250
        N_EDGES = 37500
        D = 256
        EPS = 1e-12

        def _gcn_layer(x, W, b, src, dst, norm, n_nodes):
            xt = x @ W
            msg = xt[src] * norm[:, None]
            agg = jax.ops.segment_sum(msg, dst, num_segments=n_nodes)
            return jax.nn.relu(agg + b)
        key = jax.random.key(seed)
        ks = jax.random.split(key, 10)
        h5_all = jax.random.normal(ks[0], (N_NODES, D), dtype=jnp.float32)
        edge_index = jax.random.randint(ks[1], (2, N_EDGES), 0, N_NODES, dtype=jnp.int64)
        edge_weight = jax.random.uniform(ks[2], (N_EDGES,), dtype=jnp.float32)
        s = 1.0 / np.sqrt(D)
        W6 = jax.random.normal(ks[3], (D, D), dtype=jnp.float32) * s
        b6 = jnp.zeros((D,), dtype=jnp.float32)
        W7 = jax.random.normal(ks[4], (D, D), dtype=jnp.float32) * s
        b7 = jnp.zeros((D,), dtype=jnp.float32)
        Wp = jax.random.normal(ks[5], (D, D), dtype=jnp.float32) * s
        bp = jnp.zeros((D,), dtype=jnp.float32)
        return {'h5_all': h5_all, 'edge_index': edge_index, 'edge_weight': edge_weight, 'W6': W6, 'b6': b6, 'W7': W7, 'b7': b7, 'Wp': Wp, 'bp': bp}
    _L0_gnn_all = _L0_gnn_setup()
    _L0_gnn_in = {k: v for k, v in _L0_gnn_all.items() if k in ('W6', 'b6', 'W7', 'b7', 'Wp', 'bp')}
    del _L0_gnn_all

    def _L1_gnn_setup():
        import jax, jax.numpy as jnp
        import numpy as np
        N_NODES = 12500
        N_EDGES = 400000
        CHANNEL = 256
        REDUCTION = 2
        N_GRAPHS = 64
        key = jax.random.key(seed)
        ks = jax.random.split(key, 10)
        C, R = (CHANNEL, CHANNEL // REDUCTION)
        x = jax.random.normal(ks[0], (N_NODES, C), dtype=jnp.float32)
        batch = jnp.sort(jax.random.randint(ks[1], (N_NODES,), 0, N_GRAPHS, dtype=jnp.int32))
        edge_index = jax.random.randint(ks[2], (2, N_EDGES), 0, N_NODES, dtype=jnp.int32)
        w1 = jax.random.normal(ks[3], (C, R), dtype=jnp.float32) / np.sqrt(C)
        b1 = jnp.zeros((R,), dtype=jnp.float32)
        w2 = jax.random.normal(ks[4], (R, C), dtype=jnp.float32) / np.sqrt(R)
        b2 = jnp.zeros((C,), dtype=jnp.float32)
        gcn_w = jax.random.normal(ks[5], (C, 1), dtype=jnp.float32) / np.sqrt(C)
        gcn_b = jnp.zeros((1,), dtype=jnp.float32)
        return {'x': x, 'batch': batch, 'edge_index': edge_index, 'num_graphs': N_GRAPHS, 'w1': w1, 'b1': b1, 'w2': w2, 'b2': b2, 'gcn_w': gcn_w, 'gcn_b': gcn_b}
    _L1_gnn_all = _L1_gnn_setup()
    _L1_gnn_in = {k: v for k, v in _L1_gnn_all.items() if k in ('w1', 'b1', 'w2', 'b2', 'gcn_w', 'gcn_b')}
    del _L1_gnn_all

    def _L2_gnn_setup():
        import jax, jax.numpy as jnp
        import numpy as np
        N = 6250
        E = 62500
        D = 256
        key = jax.random.key(seed)
        ks = jax.random.split(key, 12)
        s = 0.02
        x = jax.random.normal(ks[0], (N, D), dtype=jnp.float32)
        edge_index = jax.random.randint(ks[1], (2, E), 0, N, dtype=jnp.int64)
        W1 = jax.random.normal(ks[2], (D, 2 * D), dtype=jnp.float32) * s
        b1 = jax.random.normal(ks[3], (D,), dtype=jnp.float32) * s
        W2 = jax.random.normal(ks[4], (D, D), dtype=jnp.float32) * s
        b2 = jax.random.normal(ks[5], (D,), dtype=jnp.float32) * s
        w_ih = jax.random.normal(ks[6], (3 * D, D), dtype=jnp.float32) * s
        w_hh = jax.random.normal(ks[7], (3 * D, D), dtype=jnp.float32) * s
        b_ih = jax.random.normal(ks[8], (3 * D,), dtype=jnp.float32) * s
        b_hh = jax.random.normal(ks[9], (3 * D,), dtype=jnp.float32) * s
        gamma = jnp.ones((D,), dtype=jnp.float32)
        beta = jnp.zeros((D,), dtype=jnp.float32)
        return {'x': x, 'edge_index': edge_index, 'W1': W1, 'b1': b1, 'W2': W2, 'b2': b2, 'w_ih': w_ih, 'w_hh': w_hh, 'b_ih': b_ih, 'b_hh': b_hh, 'gamma': gamma, 'beta': beta}
    _L2_gnn_all = _L2_gnn_setup()
    _L2_gnn_in = {k: v for k, v in _L2_gnn_all.items() if k in ('W1', 'b1', 'W2', 'b2', 'w_ih', 'w_hh', 'b_ih', 'b_hh', 'gamma', 'beta')}
    del _L2_gnn_all

    def _L3_gnn_setup():
        import jax, jax.numpy as jnp
        import numpy as np

        def _inv_sqrt(deg):
            return jnp.where(deg > 0, jax.lax.rsqrt(deg), 0.0)
        key = jax.random.key(seed)
        k1, k2, k3, k4 = jax.random.split(key, 4)
        n_nodes, n_edges, d_in, d_half = (12500, 200000, 256, 128)
        x = jax.random.normal(k1, (n_nodes, d_in), dtype=jnp.float32)
        edge_index = jax.random.randint(k2, (2, n_edges), 0, n_nodes, dtype=jnp.int64)
        W_f = jax.random.normal(k3, (d_half, d_in), dtype=jnp.float32) * (1.0 / np.sqrt(d_in))
        W_b = jax.random.normal(k4, (d_half, d_in), dtype=jnp.float32) * (1.0 / np.sqrt(d_in))
        bias_param = jnp.zeros((2 * d_half,), dtype=jnp.float32)
        return {'x': x, 'edge_index': edge_index, 'W_f': W_f, 'W_b': W_b, 'bias_param': bias_param}
    _L3_gnn_all = _L3_gnn_setup()
    _L3_gnn_in = {k: v for k, v in _L3_gnn_all.items() if k in ('W_f', 'W_b', 'bias_param')}
    del _L3_gnn_all
    return {'x': x, 'src': src, 'dst': dst, 'edge_weight': edge_weight, 'L0_gnn_W6': _L0_gnn_in['W6'], 'L0_gnn_b6': _L0_gnn_in['b6'], 'L0_gnn_W7': _L0_gnn_in['W7'], 'L0_gnn_b7': _L0_gnn_in['b7'], 'L0_gnn_Wp': _L0_gnn_in['Wp'], 'L0_gnn_bp': _L0_gnn_in['bp'], 'L1_gnn_w1': _L1_gnn_in['w1'], 'L1_gnn_b1': _L1_gnn_in['b1'], 'L1_gnn_w2': _L1_gnn_in['w2'], 'L1_gnn_b2': _L1_gnn_in['b2'], 'L1_gnn_gcn_w': _L1_gnn_in['gcn_w'], 'L1_gnn_gcn_b': _L1_gnn_in['gcn_b'], 'L2_gnn_W1': _L2_gnn_in['W1'], 'L2_gnn_b1': _L2_gnn_in['b1'], 'L2_gnn_W2': _L2_gnn_in['W2'], 'L2_gnn_b2': _L2_gnn_in['b2'], 'L2_gnn_w_ih': _L2_gnn_in['w_ih'], 'L2_gnn_w_hh': _L2_gnn_in['w_hh'], 'L2_gnn_b_ih': _L2_gnn_in['b_ih'], 'L2_gnn_b_hh': _L2_gnn_in['b_hh'], 'L2_gnn_gamma': _L2_gnn_in['gamma'], 'L2_gnn_beta': _L2_gnn_in['beta'], 'L3_gnn_W_f': _L3_gnn_in['W_f'], 'L3_gnn_W_b': _L3_gnn_in['W_b'], 'L3_gnn_bias_param': _L3_gnn_in['bias_param']}

def reference(x, src, dst, edge_weight, L0_gnn_W6, L0_gnn_b6, L0_gnn_W7, L0_gnn_b7, L0_gnn_Wp, L0_gnn_bp, L1_gnn_w1, L1_gnn_b1, L1_gnn_w2, L1_gnn_b2, L1_gnn_gcn_w, L1_gnn_gcn_b, L2_gnn_W1, L2_gnn_b1, L2_gnn_W2, L2_gnn_b2, L2_gnn_w_ih, L2_gnn_w_hh, L2_gnn_b_ih, L2_gnn_b_hh, L2_gnn_gamma, L2_gnn_beta, L3_gnn_W_f, L3_gnn_W_b, L3_gnn_bias_param):
    import jax
    import jax.numpy as jnp

    def _L0_gnn_ref(h5_all, edge_index, edge_weight, W6, b6, W7, b7, Wp, bp):
        import jax, jax.numpy as jnp
        import numpy as np
        N_NODES = 6250
        N_EDGES = 37500
        D = 256
        EPS = 1e-12

        def _gcn_layer(x, W, b, src, dst, norm, n_nodes):
            xt = x @ W
            msg = xt[src] * norm[:, None]
            agg = jax.ops.segment_sum(msg, dst, num_segments=n_nodes)
            return jax.nn.relu(agg + b)
        src, dst = (edge_index[0], edge_index[1])
        deg_out = jax.ops.segment_sum(edge_weight, src, num_segments=N_NODES)
        deg_in = jax.ops.segment_sum(edge_weight, dst, num_segments=N_NODES)
        norm = edge_weight * jax.lax.rsqrt(deg_out[src] * deg_in[dst] + EPS)
        h6 = _gcn_layer(h5_all, W6, b6, src, dst, norm, N_NODES)
        h7 = _gcn_layer(h6, W7, b7, src, dst, norm, N_NODES)
        out = h7 @ Wp + bp
        return out

    def _L1_gnn_ref(x, batch, edge_index, num_graphs, w1, b1, w2, b2, gcn_w, gcn_b):
        import jax, jax.numpy as jnp
        import numpy as np
        N_NODES = 12500
        N_EDGES = 400000
        CHANNEL = 256
        REDUCTION = 2
        N_GRAPHS = 64
        N, C = x.shape
        seg_sum = jax.ops.segment_sum(x, batch, num_segments=num_graphs)
        cnt = jax.ops.segment_sum(jnp.ones((N,), x.dtype), batch, num_segments=num_graphs)
        chn_mean = seg_sum / jnp.maximum(cnt, 1.0)[:, None]
        gate = jax.nn.sigmoid(jax.nn.relu(chn_mean @ w1 + b1) @ w2 + b2)
        chn_se = x * gate[batch]
        h = x @ gcn_w
        loop = jnp.arange(N, dtype=edge_index.dtype)
        src = jnp.concatenate([edge_index[0], loop])
        dst = jnp.concatenate([edge_index[1], loop])
        deg = jax.ops.segment_sum(jnp.ones_like(src, dtype=x.dtype), dst, num_segments=N)
        dis = jnp.where(deg > 0, jax.lax.rsqrt(jnp.maximum(deg, 1e-12)), 0.0)
        msg = h[src] * (dis[src] * dis[dst])[:, None]
        spa = jax.nn.sigmoid(jax.ops.segment_sum(msg, dst, num_segments=N) + gcn_b)
        return x * spa + x + chn_se

    def _L2_gnn_ref(x, edge_index, W1, b1, W2, b2, w_ih, w_hh, b_ih, b_hh, gamma, beta):
        import jax, jax.numpy as jnp
        import numpy as np
        N = 6250
        E = 62500
        D = 256
        n_nodes = x.shape[0]
        row, col = (edge_index[0], edge_index[1])
        h = jnp.concatenate([x[row], x[col]], axis=-1)
        msgs = jax.nn.silu(h @ W1.T + b1) @ W2.T + b2
        agg = jax.ops.segment_sum(msgs, row, num_segments=n_nodes)
        cnt = jax.ops.segment_sum(jnp.ones((row.shape[0], 1), x.dtype), row, num_segments=n_nodes)
        agg = agg / (cnt + 1e-08)
        gi = agg @ w_ih.T + b_ih
        gh = x @ w_hh.T + b_hh
        i_r, i_z, i_n = jnp.split(gi, 3, axis=-1)
        h_r, h_z, h_n = jnp.split(gh, 3, axis=-1)
        r = jax.nn.sigmoid(i_r + h_r)
        z = jax.nn.sigmoid(i_z + h_z)
        n = jnp.tanh(i_n + r * h_n)
        x_new = (1.0 - z) * n + z * x
        mu = jnp.mean(x_new, axis=-1, keepdims=True)
        var = jnp.var(x_new, axis=-1, keepdims=True)
        return gamma * (x_new - mu) / jnp.sqrt(var + 1e-05) + beta

    def _L3_gnn_ref(x, edge_index, W_f, W_b, bias_param):
        import jax, jax.numpy as jnp
        import numpy as np

        def _inv_sqrt(deg):
            return jnp.where(deg > 0, jax.lax.rsqrt(deg), 0.0)
        n_nodes = x.shape[0]
        loops = jnp.arange(n_nodes, dtype=edge_index.dtype)
        ei = jnp.concatenate([edge_index, jnp.stack([loops, loops])], axis=1)
        n_e = ei.shape[1]
        w = jnp.ones((n_e,), dtype=x.dtype)
        col, row = (ei[0], ei[1])
        in_deg = jax.ops.segment_sum(w, col, num_segments=n_nodes)
        out_deg = jax.ops.segment_sum(w, row, num_segments=n_nodes)
        ew = _inv_sqrt(out_deg)[row] * w * _inv_sqrt(in_deg)[col]
        mf = (x @ W_f.T)[row] * ew[:, None]
        y_forward = jax.ops.segment_sum(mf, col, num_segments=n_nodes)
        mb = (x @ W_b.T)[col] * ew[:, None]
        y_backward = jax.ops.segment_sum(mb, row, num_segments=n_nodes)
        y = jnp.concatenate([y_forward, y_backward], axis=-1) + bias_param
        return y
    edge_index = jnp.stack([src, dst])
    batch0 = jnp.zeros((6250,), jnp.int32)
    x = _layernorm(x + _L0_gnn_ref(x, edge_index, edge_weight, L0_gnn_W6, L0_gnn_b6, L0_gnn_W7, L0_gnn_b7, L0_gnn_Wp, L0_gnn_bp), axis=-1)
    x = _layernorm(x + _L1_gnn_ref(x, batch0, edge_index, 64, L1_gnn_w1, L1_gnn_b1, L1_gnn_w2, L1_gnn_b2, L1_gnn_gcn_w, L1_gnn_gcn_b), axis=-1)
    x = _layernorm(x + _L2_gnn_ref(x, edge_index, L2_gnn_W1, L2_gnn_b1, L2_gnn_W2, L2_gnn_b2, L2_gnn_w_ih, L2_gnn_w_hh, L2_gnn_b_ih, L2_gnn_b_hh, L2_gnn_gamma, L2_gnn_beta), axis=-1)
    x = _layernorm(x + _L3_gnn_ref(x, edge_index, L3_gnn_W_f, L3_gnn_W_b, L3_gnn_bias_param), axis=-1)
    return x

_drawn_inputs = setup_inputs


def setup_inputs(seed=0):
    import zlib

    import numpy as np

    out = dict(_drawn_inputs(seed))
    spreads = {'L0_gnn_b6': (0.0, 0.1),
     'L0_gnn_b7': (0.0, 0.1),
     'L0_gnn_bp': (0.0, 0.1),
     'L1_gnn_b1': (0.0, 0.8),
     'L1_gnn_b2': (0.0, 0.8),
     'L2_gnn_gamma': (1.0, 0.2),
     'L2_gnn_beta': (0.0, 0.1),
     'L3_gnn_bias_param': (0.0, 0.1)}
    factors = {'L1_gnn_w1': 8.0,
     'L1_gnn_w2': 6.601,
     'L1_gnn_gcn_w': 79.835,
     'L2_gnn_W1': 5.864,
     'L2_gnn_b1': 8.0,
     'L2_gnn_W2': 5.484,
     'L2_gnn_b2': 8.0,
     'L2_gnn_w_ih': 5.087,
     'L2_gnn_b_ih': 14.847,
     'L2_gnn_b_hh': 19.602}
    for name, (base, spread) in spreads.items():
        noise = np.random.default_rng([zlib.crc32(name.encode()), seed]).standard_normal(out[name].shape)
        drawn = base * np.exp(spread * noise) if base else spread * noise
        out[name] = jnp.asarray(drawn.astype(out[name].dtype))
    for name, factor in factors.items():
        out[name] = (out[name] * factor).astype(out[name].dtype)
    return out
```

```python
from contextlib import ExitStack

import concourse.bass as bass
from concourse import mybir

ALU = mybir.AluOpType
ACT = mybir.ActivationFunctionType
AX_X = mybir.AxisListType.X
F32 = mybir.dt.float32
BF16 = mybir.dt.bfloat16
I32 = mybir.dt.int32
I16 = mybir.dt.int16
ds = bass.ds

P = 128
D = 256
GROUP = 4
RING = 8
SPAN = 24
CHUNK = 16
WORDS = 4


def apart(engine, sem):
    engine.sem_inc(sem, 1)


def in_turns(engine, turns, turn, lag):
    turn(0, True, False)
    with engine.Fori(1, turns) as i:
        turn(i, False, False)
    if lag:
        turn(turns, False, True)


def runs(g, lag, first, last):
    return g >= lag if first else g < lag if last else True


class Chain:

    def __init__(self, engine, sem):
        self.engine, self.sem, self.count, self.start = engine, sem, 0, None

    def link(self, instruction):
        instruction.then_inc(self.sem, 1)
        self.count += 1
        base = 0 if self.start is None else self.start
        self.engine.wait_ge(self.sem, base + self.count)

    def enter(self, turn, per_turn):
        self.before, self.per_turn = self.count, per_turn
        self.start, self.count = turn * per_turn + self.before, 0

    def leave(self, turns):
        assert self.count == self.per_turn, (self.count, self.per_turn)
        self.start, self.count = None, self.before + turns * self.per_turn


def build(nc, A, out):
    N, _ = A["x"].shape
    E = A["src"].shape[0]
    NB = -(-N // P)
    NBE = NB + NB % 2
    PAIRS = NBE // 2
    LAST = N - (NB - 1) * P
    J = -(-E // (P * SPAN)) * SPAN
    FULL = E // J
    TAIL = E - FULL * J
    T_MAX = (E + NB * (P - 1 + CHUNK - 1)) // P
    T = -(-T_MAX // SPAN) * SPAN
    TURNS = T // SPAN
    TG = -(-T // P)
    TC = TG * P
    GROUPS = SPAN // GROUP
    NROW = P * J // CHUNK
    ROW_PAD = NROW - P // CHUNK - 1
    assert ROW_PAD * CHUNK >= E and TAIL > 1

    rec_d = nc.dram_tensor("records_by_dst", [P * J, WORDS], F32).ap()
    rec_s = nc.dram_tensor("records_by_src", [P * J, WORDS], F32).ap()
    wt_dram = nc.dram_tensor("weights_transposed", [2, P, 2560], F32).ap()
    h6_dram = nc.dram_tensor("h6_table", [NBE * P, D], F32).ap()
    q_dram = nc.dram_tensor("q_table", [NBE * P, D], F32).ap()
    x2_dram = nc.dram_tensor("x2_table", [NBE * P, D], F32).ap()
    fwd_dram = nc.dram_tensor("fwd_table", [NBE * P, P], F32).ap()
    bwd_dram = nc.dram_tensor("bwd_table", [NBE * P, P], F32).ap()

    ctx = ExitStack()
    with ctx:
        def sb(name, shape, dt=F32):
            return ctx.enter_context(nc.sbuf_tensor(name, shape, dt))

        def sem(name):
            return ctx.enter_context(nc.semaphore(name))

        bank = [ctx.enter_context(nc.psum_tensor(f"bank{i}", [P, 512], F32)) for i in range(8)]

        NX = NBE * D
        big = sb("big", [P, 3 * NBE * D // 2])
        x_sb = big[:, 0:NX].rearrange("p (b f) -> p b f", f=D)
        p3 = big[:, :].bitcast(BF16).rearrange("p (s b f) -> p s b f", s=3, f=D)
        SP0 = NX
        spare = lambda a, n: big[:, SP0 + a:SP0 + a + n]
        d_sloc, d_sblk = spare(0, TC), spare(TC, TC)
        val_a, val_b = spare(2 * TC, TC), spare(3 * TC, TC)
        pos_start = spare(2 * TC, J).bitcast(I32)
        parts = spare(4 * TC, 2 * TC).bitcast(BF16).rearrange("p (t w) -> p t w", w=4)
        wih = spare(0, 1536).rearrange("p (k n) -> p k n", k=2)
        whh = spare(1536, 1536).rearrange("p (k n) -> p k n", k=2)
        w2t = spare(3072, 512).rearrange("p (k n) -> p k n", k=2)
        b2_bc, gamma_bc, beta_bc = (spare(3584 + D * k, D) for k in range(3))

        acc = sb("acc", [P, NBE, D + 1])
        acc_flat = acc[:, :, :].rearrange("p b f -> p (b f)")
        w_nat = acc_flat[:, 0:5120]
        w_tr = acc_flat[:, 5120:10240].rearrange("p (k n) -> p k n", k=2)
        win_s = acc_flat[:, 0:TG * 512].rearrange("p (g s w) -> p g s w", g=TG, w=WORDS)

        ring = sb("ring", [P, 2 * RING * (D + 1)])
        gbuf = ring[:, 0:RING * (D + 1)].rearrange("p (r f) -> p r f", f=D + 1)
        msg = ring[:, RING * (D + 1):].rearrange("p (r f) -> p r f", f=D + 1)
        win_d = ring[:, 0:TG * 512].rearrange("p (g s w) -> p g s w", g=TG, w=WORDS)
        tile_sums = ring[:, 0:TC * 4].rearrange("p (t w) -> p t w", w=4)
        gru_bias = ring[0:1, 0:6 * D]
        h7t = ring[:, 8 * D + 8:10 * D + 8].rearrange("p (q n) -> p q n", q=2)
        tmp_q = ring[:, 2 * RING * (D + 1) - 2 * D:].rearrange("p (q n) -> p q n", q=2)

        at = [0]

        def part(n, dt=F32):
            a = big[:, at[0]:at[0] + n]
            at[0] += n
            return a if dt == F32 else a.bitcast(dt)

        pay = part((J + RING) * WORDS).rearrange("p (j w) -> p j w", w=WORDS)
        src_i, dst_i = part(J + RING, I32), part(J + RING, I32)
        w_nat_e = part(J)
        dst_next = part(J + RING, I32)
        src_kb, dst_kb = part(J // 2, BF16), part(J // 2, BF16)
        src_blk, src_loc = part(J), part(J)
        pos_f, scan_out = part(J), part(J)
        mask = part(J // 2, BF16)
        pos_d = dst_next
        pos_s = src_i
        assert at[0] <= (NB - 1) * D

        d_idx, d_loc, d_norm = sb("d_idx", [P, TC]), sb("d_loc", [P, TC]), sb("d_norm", [P, TC])
        s_idx, s_loc = sb("s_idx", [P, TC]), sb("s_loc", [P, TC])
        blk_d, blk_s = sb("blk_d", [P, TC], I32), sb("blk_s", [P, TC], I32)
        tile_oh = sb("tile_oh", [P, TG, NB])

        oh = sb("oh", [P, 3 * GROUP, P])
        ohb = oh[:, 0:6, :].rearrange("p r n -> p (r n)").bitcast(BF16).rearrange("p (r n) -> p r n", n=P)
        oht = sb("oht", [P, 3, GROUP * P], BF16)
        stage_i = sb("stage_i", [P, 3, RING], I32)
        stage_r = sb("stage_r", [P, 3, RING, WORDS])
        staged_x, turned = sb("staged_x", [P, 2, D]), sb("turned", [P, 2, 512])
        hq = sb("hq", [P, 2, D])
        wbuf = sb("wbuf", [P, 1536])
        bias_rows = sb("bias_rows", [1, 2 * D])

        ident, ones = sb("ident", [P, P]), sb("ones", [P, P])
        ident_b, iota_b = sb("ident_b", [P, P], BF16), sb("iota_b", [P, P], BF16)
        iota_i, iota = sb("iota_i", [P, P], I32), sb("iota", [P, P])
        before = sb("before", [P, P])
        diag = hq[:, 0, :].rearrange("p (g n) -> p g n", g=2)
        tile_no_i, tile_no = sb("tile_no_i", [P, TG], I32), sb("tile_no", [P, TG])
        node_i, node_real = sb("node_i", [P, NBE], I32), sb("node_real", [P, NBE])
        sm = {n: sb(n, [P, NB + 1]) for n in (
            "tot_d", "tot_s", "incl", "off", "base_d", "base_s", "t_a", "t_b", "t_incl", "delta",
            "deg_out", "deg_in", "cnt_in", "dis", "ri", "hd", "h", "spa", "mean", "rstd", "ge")}
        sm_i = {n: sb(n, [P, NB + 1], I32) for n in ("ti_a", "ti_b")}
        row_b, blk_c, ge_sum = sb("row_b", [P, TG]), sb("blk_c", [P, TG]), sb("ge_sum", [P, TG])
        win_i_d, win_i_s = sb("win_i_d", [P, TG, 8], I32), sb("win_i_s", [P, TG, 8], I32)
        table3 = sb("table3", [P, 3, NB + 1], BF16)
        viol, flag_i = sb("viol", [P, 1]), sb("flag_i", [P, 1], I32)
        stats, mv_one, mv = sb("stats", [P, 2, 6]), sb("mv_one", [P, 2, 2]), sb("mv", [P, NBE, 2])
        cols = sb("cols", [P, 16])
        gw_bc, gate_bc, bias_bc = sb("gw_bc", [P, D]), sb("gate_bc", [P, D]), sb("bias_bc", [P, D])
        junk = sb("junk", [P, 4, 64])
        zeros = gate_bc
        SG_T, SG_S = (2, 3, 6), (4, 5, 7)
        rz = oh[:, 0:8, :].rearrange("p r n -> p (r n)").rearrange("p (q n) -> p q n", q=2)
        n_sb = oh[:, 8:12, :].rearrange("p r n -> p (r n)").rearrange("p (q n) -> p q n", q=2)
        cnt_c = sb("cnt_c", [P, 2, 2])

        names = """consts pads_set edges_in weights_in wt_turned wt_copied wt_stored dve_chain pe_chain waited pool_waited
        act_chain totals_ready prefix_done flag_sum flag_ready win_d_ready win_s_ready records_ready
        diag_ready blk_bcast slow_pos pos_s_ready scat_staged rec_d_done win_d_in
        win_s_in win_turned win_copied arrays_ready deg_oh deg_mm deg_done
        comb_v comb_t comb_c comb_s comb_done seg_oh seg_mm seg_cp seg_ready
        sg_oh sg_t sg_cp sg_mm sg_sel sg_ready l0_ready staged one_hot mm accd
        d_staged d_t d_at d_m d_h d_m2 d_h7 d_res x_in var_ready rstd_ready wb_in consts_in
        col_ready col_done gate_step gate_done spa_in spa_out pass_ready p_loaded p_split
        l2_oh l2_t l2_cp l2_p l2_add l2_silu l2_c l2_acc sqrt_in sqrt_out x2_done
        g_agg g_t1 g_a1 g_m g_ag2 g_t2 g_a2 g_ab g_rz g_n g_tanh g_xn g_done final_ready
        f_res f_out gw_in w5_in y_ready prep prep_done""".split()
        S = {n: sem(n) for n in names}
        gd = [sem(f"gathered{i}") for i in range(RING)]
        sc = [sem(f"scattered{i}") for i in range(RING)]
        pair = {n: [sem(f"{n}{q}") for q in range(2)] for n in ("h_out", "x2_in", "x2b_in", "tab_out", "fin_in", "p_in", "y_out")}
        block = ctx.enter_context(nc.Block())

        W_OFF = {"W1": 0, "W2": 512, "ih": 768, "hh": 1536, "F": 2304, "B": 2432}
        NAT = {"W1": (0, 2, 512), "W2": (1024, 2, 256), "ih": (1536, 6, 256), "hh": (3072, 6, 256),
               "F": (4608, 1, 256), "B": (4864, 1, 256)}
        TURN = []
        for name, (a, rows, width) in NAT.items():
            for r in range(rows):
                for c in range(width // P):
                    half = D // P if name == "W1" else 0
                    o = W_OFF[name] + r * P + (c // 2 * D if half else 0)
                    TURN.append((a + r * width + c * P, c % 2, o))

        def dense_rows(dram, block_no):
            return dram[ds(block_no * P, P), :]

        @block.sync
        def _(sp):
            views = {"W1": A["L2_gnn_W1"], "W2": A["L2_gnn_W2"], "ih": A["L2_gnn_w_ih"],
                     "hh": A["L2_gnn_w_hh"], "F": A["L3_gnn_W_f"], "B": A["L3_gnn_W_b"]}
            sp.wait_ge(S["pads_set"], 4)
            CUT = FULL // 16 * 16
            for lo, hi in ((0, CUT), (CUT, FULL)):
                for t, a in ((src_i, "src"), (dst_i, "dst"), (w_nat_e, "edge_weight")):
                    sp.dma_start(t[lo:hi, 0:J], A[a][lo * J:hi * J].rearrange("(p j) -> p j", j=J)).then_inc(S["edges_in"], 16)
                sp.dma_start(dst_next[lo:hi, 0:J], A["dst"][lo * J + 1:hi * J + 1].rearrange("(p j) -> p j", j=J)).then_inc(S["edges_in"], 16)
            for t, a in ((src_i, "src"), (dst_i, "dst"), (w_nat_e, "edge_weight")):
                sp.dma_start(t[FULL:FULL + 1, 0:TAIL], A[a][FULL * J:E].rearrange("(p j) -> p j", p=1)).then_inc(S["edges_in"], 16)
            sp.dma_start(dst_next[FULL:FULL + 1, 0:TAIL - 1], A["dst"][FULL * J + 1:E].rearrange("(p j) -> p j", p=1)).then_inc(S["edges_in"], 16)
            for name, (a, rows, width) in NAT.items():
                sp.dma_start(w_nat[:, a:a + rows * width].rearrange("p (r n) -> p r n", r=rows),
                             views[name].rearrange("(r p) n -> p r n", p=P)).then_inc(S["weights_in"], 16)
            sp.dma_start(wbuf[:, 0:512].rearrange("p (k n) -> p k n", k=2), A["L0_gnn_W6"].rearrange("(k p) n -> p k n", p=P)).then_inc(S["consts_in"], 16)
            bias = {"L0_gnn_b6": 0, "L0_gnn_bp": D}
            for n, o in bias.items():
                sp.dma_start(bias_rows[0:1, o:o + D], A[n].rearrange("(a n) -> a n", a=1)).then_inc(S["consts_in"], 16)
            for k in range(2):
                sp.dma_start(cols[:, k:k + 1], A["L0_gnn_b7"][k * P:(k + 1) * P].rearrange("(p a) -> p a", a=1)).then_inc(S["consts_in"], 16)
            sp.dma_start(cols[:, 2:3], A["L1_gnn_b1"].rearrange("(p a) -> p a", a=1)).then_inc(S["consts_in"], 16)
            sp.dma_start(cols[:, 3:4], A["L1_gnn_gcn_b"].partition_broadcast(P)).then_inc(S["consts_in"], 16)
            sp.dma_start(gw_bc[:, :], A["L1_gnn_gcn_w"].rearrange("n a -> (a n)").partition_broadcast(P)).then_inc(S["consts_in"], 16)
            sp.dma_start(bias_bc[:, :], A["L3_gnn_bias_param"].partition_broadcast(P)).then_inc(S["consts_in"], 16)
            sp.wait_ge(S["wt_copied"], len(TURN))
            for k in range(2):
                sp.dma_start(wt_dram[k], w_tr[:, k, :]).then_inc(S["wt_stored"], 16)
            sp.wait_ge(S["l0_ready"], 1)
            sp.wait_ge(S["scat_staged"], 2 * (J // RING + 1))
            sp.dma_start(x_sb[:, 0:NB - 1, :], A["x"][0:(NB - 1) * P, :].rearrange("(b p) f -> p b f", p=P)).then_inc(S["x_in"], 16)
            sp.dma_start(x_sb[0:LAST, NB - 1, :], A["x"][(NB - 1) * P:N, :]).then_inc(S["x_in"], 16)

            def store_h6(i, q):
                sp.wait_ge(S["d_h"], i * 2 + q + 1 + 2)
                sp.dma_start(dense_rows(h6_dram, i * 2 + q), hq[:, q, :]).then_inc(pair["h_out"][q], 16)
            with sp.Fori(0, PAIRS) as i:
                for q in range(2):
                    store_h6(i, q)
            sp.wait_ge(S["d_m"], NBE + 2)
            sp.dma_start(wbuf[:, 0:512].rearrange("p (k n) -> p k n", k=2), A["L0_gnn_W7"].rearrange("(k p) n -> p k n", p=P)).then_inc(S["wb_in"], 16)
            sp.dma_start(wbuf[:, 512:1024].rearrange("p (k n) -> p k n", k=2), A["L0_gnn_Wp"].rearrange("(k p) n -> p k n", p=P)).then_inc(S["wb_in"], 16)
            sp.wait_ge(S["d_m2"], NBE + 2)
            sp.dma_start(wbuf[:, 0:256].rearrange("p (k n) -> p k n", k=2), A["L1_gnn_w1"].rearrange("(k p) n -> p k n", p=P)).then_inc(S["wb_in"], 16)
            sp.dma_start(wbuf[:, 256:512], A["L1_gnn_w2"]).then_inc(S["wb_in"], 16)
            sp.dma_start(bias_rows[0:1, 0:D], A["L1_gnn_b2"].rearrange("(a n) -> a n", a=1)).then_inc(S["wb_in"], 16)
            sp.dma_start(bias_rows[0:1, D:2 * D], A["L2_gnn_b1"].rearrange("(a n) -> a n", a=1)).then_inc(S["wb_in"], 16)
            sp.wait_ge(S["gate_done"], 1)
            sp.wait_ge(S["wt_stored"], 32)
            sp.dma_start(wbuf[:, 0:1024].rearrange("p (k n) -> p k n", k=2), wt_dram[:, :, 0:512].rearrange("k p n -> p k n")).then_inc(S["wb_in"], 16)
            sp.wait_ge(S["x2_done"], 1)
            sp.dma_start(x2_dram.rearrange("(b p) f -> p b f", p=P), x_sb).then_inc(S["p_loaded"], 16)
            sp.wait_ge(S["p_loaded"], 16)

            def load_pair(i):
                for q in range(2):
                    sp.wait_ge(S["d_t"], i * 2 + q + 1 + 2 * NBE)
                    sp.dma_start(staged_x[:, q, :], dense_rows(x2_dram, i * 2 + q)).then_inc(pair["p_in"][q], 16)

            def store_q(i):
                for q in range(2):
                    sp.wait_ge(S["d_h"], i * 2 + q + 3 + NBE)
                    sp.dma_start(dense_rows(q_dram, i * 2 + q), hq[:, q, :]).then_inc(pair["tab_out"][q], 16)

            load_pair(0)
            with sp.Fori(1, PAIRS) as i:
                load_pair(i)
                store_q(i - 1)
            store_q(PAIRS - 1)
            sp.wait_ge(S["g_done"], 1)
            sp.dma_start(wih, wt_dram[:, :, 768:1536].rearrange("k p n -> p k n")).then_inc(S["w5_in"], 16)
            sp.dma_start(whh, wt_dram[:, :, 1536:2304].rearrange("k p n -> p k n")).then_inc(S["w5_in"], 16)
            sp.dma_start(w2t, wt_dram[:, :, 512:768].rearrange("k p n -> p k n")).then_inc(S["w5_in"], 16)
            for t, n in ((b2_bc, "L2_gnn_b2"), (gamma_bc, "L2_gnn_gamma"), (beta_bc, "L2_gnn_beta")):
                sp.dma_start(t, A[n].partition_broadcast(P)).then_inc(S["w5_in"], 16)
            sp.dma_start(wbuf[:, 0:512].rearrange("p (k n) -> p k n", k=2), wt_dram[:, :, 2304:2560].rearrange("k p n -> p k n")).then_inc(S["w5_in"], 16)
            for k, n in enumerate(("L2_gnn_b_ih", "L2_gnn_b_hh")):
                sp.dma_start(gru_bias[:, 3 * D * k:3 * D * (k + 1)], A[n].rearrange("(a n) -> a n", a=1)).then_inc(S["w5_in"], 16)
            with sp.Fori(0, PAIRS) as i:
                for q in range(2):
                    sp.wait_ge(S["g_xn"], i * 2 + q + 1)
                    sp.dma_start(hq[:, q, :], dense_rows(x2_dram, i * 2 + q)).then_inc(pair["x2_in"][q], 16)
            sp.wait_ge(S["g_xn"], NBE + 2)
            with sp.Fori(0, PAIRS) as i:
                for q in range(2):
                    sp.wait_ge(S["f_res"], i * 2 + q + 1)
                    sp.dma_start(hq[:, q, :], dense_rows(x2_dram, i * 2 + q)).then_inc(pair["x2b_in"][q], 16)
            sp.wait_ge(S["f_res"], NBE + 2)
            with sp.Fori(0, PAIRS) as i:
                for q in range(2):
                    n = i * 2 + q
                    sp.wait_ge(S["d_h"], n + 3 + 2 * NBE)
                    sp.dma_start(dense_rows(fwd_dram, n), hq[:, q, 0:P]).then_inc(pair["tab_out"][q], 16)
                    sp.dma_start(dense_rows(bwd_dram, n), hq[:, q, P:D]).then_inc(pair["tab_out"][q], 16)
            sp.wait_ge(S["final_ready"], 1)
            with sp.Fori(0, PAIRS) as i:
                for q in range(2):
                    n = i * 2 + q
                    sp.wait_ge(S["f_out"], n + 1)
                    sp.dma_start(hq[:, q, 0:P], dense_rows(fwd_dram, n)).then_inc(pair["fin_in"][q], 16)
                    sp.dma_start(hq[:, q, P:D], dense_rows(bwd_dram, n)).then_inc(pair["fin_in"][q], 16)
            with sp.Fori(0, PAIRS - 1) as i:
                for q in range(2):
                    sp.wait_ge(S["y_ready"], i * 2 + q + 1)
                    sp.dma_start(dense_rows(out, i * 2 + q), staged_x[:, q, :]).then_inc(pair["y_out"][q], 16)
            sp.wait_ge(S["y_ready"], 2 * (PAIRS - 1) + 1)
            sp.dma_start(out[(NB - 1) * P:N, :], staged_x[0:LAST, 0, :]).then_inc(pair["y_out"][0], 16)
            sp.wait_ge(pair["y_out"][0], 16 * PAIRS)
            sp.wait_ge(pair["y_out"][1], 16 * (PAIRS - 1))

        @block.gpsimd
        def _(pool):
            pool.memset(ident[:, :], 0.0).then_inc(S["consts"], 1)
            pool.memset(ones[:, :], 1.0).then_inc(S["consts"], 1)
            pool.memset(before[:, :], 1.0).then_inc(S["consts"], 1)
            pool.wait_ge(S["consts"], 3)
            pool.affine_select(out=ident[:, :], in_=ident[:, :], compare_op=ALU.not_equal, fill=1.0, base=0,
                               pattern=[[-1, P]], channel_multiplier=1).then_inc(S["consts"], 1)
            pool.affine_select(out=before[:, :], in_=before[:, :], compare_op=ALU.is_gt, fill=0.0, base=0,
                               pattern=[[1, P]], channel_multiplier=-1).then_inc(S["consts"], 1)
            pool.iota(iota_i[:, :], pattern=[[1, P]], base=0, channel_multiplier=0).then_inc(S["consts"], 1)
            pool.iota(tile_no_i[:, :], pattern=[[P, TG]], base=0, channel_multiplier=1).then_inc(S["consts"], 1)
            pool.iota(node_i[:, :], pattern=[[P, NBE]], base=0, channel_multiplier=1).then_inc(S["consts"], 1)
            pool.iota(pos_start[:, :], pattern=[[1, J]], base=0, channel_multiplier=J).then_inc(S["consts"], 1)

            def windows(rec, index, win, done):
                rows = rec.rearrange("(r s) w -> r (s w)", s=CHUNK)
                flat = win.rearrange("p g s w -> p g (s w)")
                for g in range(TG):
                    for k in range(P // CHUNK):
                        w = CHUNK * WORDS
                        pool.indirect_dma_start(out=flat[:, g, k * w:(k + 1) * w], out_offset=None, in_=rows,
                                                in_offset=bass.IndirectOffsetOnAxis(ap=index[:, g, k:k + 1], axis=0)).then_inc(done, 16)

            pool.wait_ge(S["flag_ready"], 1)
            unsorted = pool.value_load(flag_i[0:1, 0:1], min_val=0, max_val=E)
            with pool.If(unsorted > 0):
                pool.wait_ge(S["slow_pos"], 1)

                def scatter_slowly(j, first):
                    if not first:
                        pool.wait_ge(S["rec_d_done"], j * 16)
                    pool.tensor_copy(stage_i[:, 0, 0:1], pos_d[:, ds(j, 1)]).then_inc(S["slow_pos"], 1)
                    pool.tensor_copy(stage_r[:, 0, 0, :], pay[:, ds(j, 1), :].rearrange("p a w -> p (a w)")).then_inc(S["slow_pos"], 1)
                    pool.wait_ge(S["slow_pos"], j * 2 + 3)
                    apart(pool, S["pool_waited"])
                    pool.indirect_dma_start(out=rec_d, out_offset=bass.IndirectOffsetOnAxis(ap=stage_i[:, 0, 0:1], axis=0),
                                            in_=stage_r[:, 0, 0, :], in_offset=None).then_inc(S["rec_d_done"], 16)

                scatter_slowly(0, True)
                with pool.Fori(1, J) as j:
                    scatter_slowly(j, False)
                pool.wait_ge(S["rec_d_done"], J * 16)
            with pool.Else():
                pool.dma_start(rec_d.rearrange("(p j) w -> p (j w)", j=J), pay[:, 0:J, :].rearrange("p j w -> p (j w)")).then_inc(S["rec_d_done"], 16)
                pool.wait_ge(S["rec_d_done"], 16)
            pool.wait_ge(S["win_d_ready"], 1)
            windows(rec_d, win_i_d, win_d, S["win_d_in"])

            def stage_scatter(first, v):
                pool.tensor_copy(stage_i[:, v, :], pos_s[:, ds(first, RING)]).then_inc(S["scat_staged"], 1)
                pool.tensor_copy(stage_r[:, v, :, :], pay[:, ds(first, RING), :]).then_inc(S["scat_staged"], 1)

            def scatter_turn(i, first):
                for v in range(3):
                    pool.wait_ge(S["scat_staged"], i * 6 + 2 * v + 2)
                    apart(pool, S["pool_waited"])
                    for u in range(RING):
                        if not (first and v == 0):
                            pool.wait_ge(sc[u], i * 48 + 16 * v)
                            apart(pool, S["pool_waited"])
                        pool.indirect_dma_start(out=rec_s, out_offset=bass.IndirectOffsetOnAxis(ap=stage_i[:, v, u:u + 1], axis=0),
                                                in_=stage_r[:, v, u, :], in_offset=None).then_inc(sc[u], 16)
                        if u == RING // 2 - 1:
                            stage_scatter(i * SPAN + RING * (v + 1), (v + 1) % 3)

            turns = J // SPAN
            pool.wait_ge(S["pos_s_ready"], 1)
            stage_scatter(0, 0)
            scatter_turn(0, True)
            with pool.Fori(1, turns) as i:
                scatter_turn(i, False)
            for u in range(RING):
                pool.wait_ge(sc[u], 48 * turns)
            pool.wait_ge(S["win_s_ready"], 1)
            pool.wait_ge(S["wt_stored"], 32)
            windows(rec_s, win_i_s, win_s, S["win_s_in"])

            def gathers(k, table, width, index, free, base, together=1):
                def stage(first, v):
                    pool.tensor_copy(stage_i[:, v, :], index[:, ds(first, RING)]).then_inc(S["staged"], 1)

                rounds = (T // RING + 1) * k
                if k:
                    pool.wait_ge(S["staged"], rounds)
                stage(0, 0)
                with pool.Fori(0, TURNS) as i:
                    for u in range(SPAN):
                        v = u // RING
                        if u % RING == 0:
                            pool.wait_ge(S["staged"], i * 3 + rounds + v + 1)
                        pool.wait_ge(free, i * (SPAN // together) + base + u // together + 1)
                        apart(pool, S["pool_waited"])
                        pool.indirect_dma_start(out=gbuf[:, u % RING, 0:width], out_offset=None, in_=table,
                                                in_offset=bass.IndirectOffsetOnAxis(ap=stage_i[:, v, u % RING:u % RING + 1], axis=0)).then_inc(gd[u % RING], 16)
                        if u % RING == RING // 2 - 1:
                            stage(i * SPAN + RING * (v + 1), (v + 1) % 3)

            pool.wait_ge(S["l0_ready"], 1)
            pool.wait_ge(S["scat_staged"], 2 * (J // RING + 1))
            gathers(0, A["x"], D, d_idx, S["mm"], 0)
            for q in range(2):
                pool.wait_ge(pair["h_out"][q], 16 * PAIRS)
            gathers(1, h6_dram, D, d_idx, S["mm"], T)
            for q in range(2):
                pool.wait_ge(pair["tab_out"][q], 16 * PAIRS)
            gathers(2, q_dram, D, s_idx, S["l2_add"], 0, 2)
            for q in range(2):
                pool.wait_ge(pair["tab_out"][q], 48 * PAIRS)
            gathers(3, fwd_dram, P, s_idx, S["mm"], 2 * T)
            gathers(4, bwd_dram, P, d_idx, S["mm"], 3 * T)

        @block.tensor
        def _(pe):
            regs = [pe.alloc_register(f"pe_blk{j}") for j in range(8)]
            pe.sem_inc(S["mm"], 8)
            pe.sem_inc(S["seg_mm"], 8)
            pe.sem_inc(S["deg_mm"], 4)
            pe.sem_inc(S["sg_t"], 3)
            pe.sem_inc(S["sg_mm"], 3)
            pe.sem_inc(S["d_t"], 2)
            pe.sem_inc(S["d_m"], 2)
            pe.sem_inc(S["d_m2"], 2)
            pe.sem_inc(S["l2_p"], 4)
            pe.sem_inc(S["l2_c"], 12)
            for n in ("g_t1", "g_m", "g_t2", "g_ab"):
                pe.sem_inc(S[n], 2)

            pe.wait_ge(S["consts"], 9)
            pe.wait_ge(S["weights_in"], 16 * len(NAT))
            for m, (a, _, _) in enumerate(TURN):
                if m >= 4:
                    pe.wait_ge(S["wt_copied"], m - 3)
                pe.transpose(bank[4 + m % 4][:, 0:P], w_nat[:, a:a + P], ident[:, :]).then_inc(S["wt_turned"], 1)
            pe.wait_ge(S["totals_ready"], 1)
            for k, tot in enumerate((sm["tot_d"], sm["tot_s"])):
                pe.matmul(bank[k][:, 0:NB], before[:, :], tot[:, 0:NB], start=True, stop=True)
                pe.matmul(bank[k][:, 64:64 + NB], ones[:, :], tot[:, 0:NB], start=True, stop=True)
            pe.matmul(bank[1][:, 128:129], ones[:, :], viol[:, :], start=True, stop=True).then_inc(S["prefix_done"], 1)
            for k in range(2):
                for g in range(TG):
                    pe.wait_ge(S["diag_ready"], k * TG + g + 1)
                    pe.matmul(bank[2 + g // 4][:, g % 4 * P:(g % 4 + 1) * P], ones[:, :], diag[:, g % 2, :],
                              start=True, stop=True).then_inc(S["blk_bcast"], 1)

            def turn_windows(win, words, done, fills):
                pe.wait_ge(done, 16 * TG * (P // CHUNK))
                for w in range(words):
                    for lo in range(0, TG, 4):
                        b = 4 + fills % 4
                        pe.wait_ge(S["wt_copied"], len(TURN) + fills - 3)
                        for g in range(lo, min(lo + 4, TG)):
                            mm = pe.transpose(bank[b][:, (g - lo) * P:(g - lo + 1) * P], win[:, g, :, w], ident[:, :])
                        mm.then_inc(S["win_turned"], 1)
                        fills += 1
                return fills

            fills = turn_windows(win_d, 3, S["win_d_in"], 0)

            def segment_sums(k):
                pe.wait_ge(S["seg_ready"], k + 1)
                with pe.Fori(0, T // 8) as i:
                    for u in range(8):
                        n = i * 8 + T * k + u
                        if u % 4 == 0:
                            pe.wait_ge(S["seg_cp"], i * 2 + T // 4 * k + u // 4 + 1)
                        pe.wait_ge(S["seg_oh"], n + 1)
                        pe.matmul(bank[2 + u // 4][:, u % 4 * 4:u % 4 * 4 + 4], ohb[:, u, :],
                                  parts[:, ds(i * 8 + u, 1), :].rearrange("p a w -> p (a w)"), start=True, stop=True).then_inc(S["seg_mm"], 1)

            def combine(k, turns):
                for g in range(TG):
                    pe.wait_ge(S["comb_v"], k + 1)
                    mm = pe.transpose(bank[4 + g // 4][:, g % 4 * P:(g % 4 + 1) * P], val_b[:, g * P:(g + 1) * P], ident[:, :])
                    if g in (3, TG - 1):
                        mm.then_inc(S["comb_t"], 1)
                pe.wait_ge(S["comb_c"], 2 * k + 2)
                for g in range(TG):
                    mm = pe.matmul(bank[1][:, 0:NB], val_a[:, g * P:(g + 1) * P], tile_oh[:, g, :], start=(g == 0), stop=(g == TG - 1))
                mm.then_inc(S["comb_done"], 1)

            segment_sums(0)
            combine(0, 0)
            combine(1, 0)
            pe.matmul(bank[0][:, 0:NB], ones[:, :], zeros[:, 0:NB], start=True, stop=False, skip_group_check=True)
            with pe.Fori(0, J // 8) as i:
                for u in range(8):
                    pe.wait_ge(S["deg_oh"], i * 8 + u + 1)
                    pe.matmul(bank[0][:, 0:NB], oh[:, 4 + u % 4, :], junk[:, u % 4, 0:NB], start=False, stop=False,
                              skip_group_check=True).then_inc(S["deg_mm"], 1)

            def node_values(k):
                pe.wait_ge(S["sg_ready"], k + 1)

                def turn_of(i, first, last):
                    for g in range(2 if last else GROUPS):
                        m = i * GROUPS + T // GROUP * k + g
                        if not last:
                            pe.wait_ge(S["sg_oh"], i * SPAN + T * k + 4 * g + 4)
                            pe.wait_ge(S["sg_cp"], m + 1)
                            b = bank[SG_T[g % 3]][:, 0:256].bitcast(BF16)
                            for u in range(GROUP):
                                mm = pe.transpose(b[:, u * P:(u + 1) * P], ohb[:, g % 3 * GROUP + u, :], ident_b[:, :])
                            mm.then_inc(S["sg_t"], 1)
                        if runs(g, 2, first, last):
                            h = (g - 2) % 3
                            pe.wait_ge(S["sg_cp"], m - 2 + 1 + 3)
                            pe.wait_ge(S["sg_sel"], m - 2 + 1)
                            for u in range(GROUP):
                                for s in range(3):
                                    mm = pe.matmul(bank[SG_S[h]][:, u * 64:u * 64 + NB], oht[:, h, u * P:(u + 1) * P], table3[:, s, 0:NB],
                                                   start=(s == 0), stop=(s == 2))
                            mm.then_inc(S["sg_mm"], 1)

                in_turns(pe, TURNS, turn_of, 2)
                pe.wait_ge(S["sg_sel"], T // GROUP * (k + 1) + 3)

            node_values(0)
            node_values(1)
            fills = turn_windows(win_s, 2, S["win_s_in"], fills)

            def scatter_pass(k, kk, width):
                with pe.Fori(0, TURNS) as i:
                    for u in range(SPAN):
                        n = i * SPAN + T * kk + u
                        pe.wait_ge(S["one_hot"], n + 1)
                        pe.wait_ge(gd[u % RING], i * 48 + 16 * (T // RING * k + u // RING + 1))
                        pe.wait_ge(S["accd"], n + 1)
                        pe.matmul(bank[u % 4][:, 0:width], oh[:, u % 4, :], gbuf[:, u % RING, 0:width],
                                  start=True, stop=True).then_inc(S["mm"], 1)

            def turn(n, q, src, b):
                for k in range(2):
                    mm = pe.transpose(bank[b][:, k * P:(k + 1) * P], src[:, k * P:(k + 1) * P], ident[:, :])
                mm.then_inc(S["d_t"], 1)

            w0, w1 = (wbuf[:, 512 * k:512 * (k + 1)].rearrange("p (k n) -> p k n", k=2) for k in range(2))
            scatter_pass(0, 0, D)
            pe.wait_ge(S["consts_in"], 16 * 9)
            with pe.Fori(0, PAIRS) as i:
                for q in range(2):
                    n = i * 2 + q
                    pe.wait_ge(S["d_staged"], n + 1)
                    pe.wait_ge(S["d_at"], n + 1)
                    turn(n, q, staged_x[:, q, :], 4 + q)
                for q in range(2):
                    n = i * 2 + q
                    pe.wait_ge(S["d_at"], n + 1 + 2)
                    pe.wait_ge(S["d_h"], n + 1)
                    for k in range(2):
                        pe.matmul(bank[6 + q][:, 0:D], turned[:, q, k * P:(k + 1) * P], w0[:, k, :], start=(k == 0), stop=False)
                    pe.matmul(bank[6 + q][:, 0:D], ones[0:1, :], bias_rows[0:1, 0:D], start=False, stop=True).then_inc(S["d_m"], 1)
            scatter_pass(1, 1, D)
            pe.wait_ge(S["wb_in"], 32)
            with pe.Fori(0, PAIRS) as i:
                for q in range(2):
                    n = i * 2 + q + NBE
                    pe.wait_ge(S["d_staged"], n + 1)
                    pe.wait_ge(S["d_at"], n + 1)
                    turn(n, q, staged_x[:, q, :], 4 + q)
                for q in range(2):
                    n = i * 2 + q + NBE
                    pe.wait_ge(S["d_at"], n + 1 + 2)
                    pe.wait_ge(S["d_h7"], i * 2 + q + 1)
                    for o in range(2):
                        for k in range(2):
                            mm = pe.matmul(bank[6 + q][:, o * P:(o + 1) * P], w0[:, k, o * P:(o + 1) * P], turned[:, q, k * P:(k + 1) * P],
                                           start=(k == 0), stop=(k == 1))
                    mm.then_inc(S["d_m"], 1)
                for q in range(2):
                    n = i * 2 + q
                    pe.wait_ge(S["d_h7"], n + 1 + 2)
                    pe.wait_ge(S["d_res"], n + 1)
                    for k in range(2):
                        pe.matmul(bank[2 + q][:, 0:D], h7t[:, q, k * P:(k + 1) * P], w1[:, k, :], start=(k == 0), stop=False)
                    pe.matmul(bank[2 + q][:, 0:D], ones[0:1, :], bias_rows[0:1, D:2 * D], start=False, stop=True).then_inc(S["d_m2"], 1)
            pe.matmul(bank[0][0:1, 256:256 + D], ones[:, 0:1], zeros[:, :], start=True, stop=False, skip_group_check=True)
            with pe.Fori(0, NBE) as b:
                pe.wait_ge(S["col_ready"], b + 1)
                pe.matmul(bank[0][0:1, 256:256 + D], ones[:, 0:1], x_sb[:, ds(b, 1), :].rearrange("p a f -> p (a f)"),
                          start=False, stop=False, skip_group_check=True).then_inc(S["col_done"], 1)
            pe.wait_ge(S["wb_in"], 32 + 64)
            pe.wait_ge(S["gate_step"], 1)
            for k in range(2):
                mm = pe.matmul(bank[1][:, k:k + 1], staged_x[0:1, 0, k * P:(k + 1) * P], ones[0:1, 0:1], start=True, stop=True)
            mm.then_inc(S["pe_chain"], 1)
            pe.wait_ge(S["gate_step"], 2)
            for k in range(2):
                mm = pe.matmul(bank[1][:, 4:5], wbuf[:, k * P:(k + 1) * P], cols[:, 4 + k:5 + k], start=(k == 0), stop=(k == 1))
            mm.then_inc(S["pe_chain"], 1)
            pe.wait_ge(S["gate_step"], 3)
            pe.matmul(bank[1][0:1, 128:128 + D], cols[:, 6:7], wbuf[:, 256:512], start=True, stop=False)
            pe.matmul(bank[1][0:1, 128:128 + D], ones[0:1, 0:1], bias_rows[0:1, 0:D], start=False, stop=True).then_inc(S["pe_chain"], 1)
            pe.wait_ge(S["gate_step"], 4)
            pe.matmul(bank[4][:, 0:D], ones[0:1, :], staged_x[0:1, 1, :], start=True, stop=True).then_inc(S["pe_chain"], 1)

            node_values(2)
            segment_sums(1)
            combine(2, 0)

            pe.wait_ge(S["wb_in"], 32 + 64 + 16)
            w_ab = wbuf[:, 0:1024].rearrange("p (k n) -> p k n", k=2)
            with pe.Fori(0, PAIRS) as i:
                for q in range(2):
                    n = i * 2 + q + 2 * NBE
                    pe.wait_ge(pair["p_in"][q], i * 16 + 16)
                    pe.wait_ge(S["d_at"], n + 1)
                    turn(n, q, staged_x[:, q, :], 4 + q)
                for q in range(2):
                    n = i * 2 + q
                    pe.wait_ge(S["d_at"], n + 1 + 2 + 2 * NBE)
                    pe.wait_ge(S["d_h"], n + 1 + NBE)
                    pe.wait_ge(S["p_split"], n + 1)
                    for k in range(2):
                        pe.matmul(bank[2 + q][:, 0:D], turned[:, q, k * P:(k + 1) * P], w_ab[:, k, D:2 * D], start=(k == 0), stop=(k == 1))
                    for k in range(2):
                        pe.matmul(bank[6 + q][:, 0:D], turned[:, q, k * P:(k + 1) * P], w_ab[:, k, 0:D], start=(k == 0), stop=False)
                    pe.matmul(bank[6 + q][:, 0:D], ones[0:1, :], bias_rows[0:1, D:2 * D], start=False, stop=True).then_inc(S["d_m"], 1)

            pe.wait_ge(S["pass_ready"], 1)

            def l2_products(i, first, last):
                for g in range(2 if last else GROUPS):
                    m = i * GROUPS + g
                    if runs(g, 1, first, last):
                        h = g - 1
                        if h % 2 == 0:
                            pe.load(regs, blk_s[0:1, ds(i * SPAN + 4 * h, 8)])
                        pe.wait_ge(S["l2_cp"], m - 1 + 1 + 2)
                        for u in range(GROUP):
                            b = pe.snap(regs[4 * (h % 2) + u], min_val=0, max_val=NB - 1)
                            if u % 2 == 0:
                                pe.wait_ge(S["l2_add"], i * (SPAN // 2) + 2 * h + u // 2 + 3)
                            for s in range(3):
                                mm = pe.matmul(bank[2 + u // 2][:, u % 2 * D:(u % 2 + 1) * D], oht[:, h % 2, u * P:(u + 1) * P],
                                               p3[:, s, ds(b, 1), :].rearrange("p a f -> p (a f)"), start=(s == 0), stop=(s == 2))
                            if u % 2:
                                mm.then_inc(S["l2_p"], 1)
                    if not last:
                        pe.wait_ge(S["l2_oh"], i * SPAN + 4 * g + 4)
                        pe.wait_ge(S["l2_cp"], m + 1)
                        for u in range(GROUP):
                            mm = pe.transpose(bank[g % 2][:, u * P:(u + 1) * P], oh[:, (4 * g + u) % 12, :], ident[:, :])
                        mm.then_inc(S["l2_t"], 1)
                    if runs(g, 2, first, last):
                        for u in range(GROUP):
                            t = 4 * (g - 2) + u
                            pe.wait_ge(S["l2_silu"], i * (SPAN // 2) + t // 2 + 1)
                            pe.wait_ge(S["l2_acc"], i * SPAN + t + 1)
                            pe.matmul(bank[4 + u][:, 0:D + 1], oh[:, t % 12, :], msg[:, t % RING, :], start=True, stop=True).then_inc(S["l2_c"], 1)

            in_turns(pe, TURNS, l2_products, 2)

            pe.wait_ge(S["w5_in"], 16 * 9)
            with pe.Fori(0, PAIRS) as i:
                for q in range(2):
                    n = i * 2 + q
                    pe.wait_ge(S["g_agg"], n + 1)
                    pe.wait_ge(S["g_a1"], n + 1)
                    pe.wait_ge(S["g_ag2"], n + 1)
                    for k in range(2):
                        mm = pe.transpose(bank[q][:, k * P:(k + 1) * P], staged_x[:, q, k * P:(k + 1) * P], ident[:, :])
                    mm.then_inc(S["g_t1"], 1)
                for q in range(2):
                    n = i * 2 + q
                    pe.wait_ge(S["g_a1"], n + 1 + 2)
                    for k in range(2):
                        mm = pe.matmul(bank[q][:, D:2 * D], h7t[:, q, k * P:(k + 1) * P], w2t[:, k, :], start=(k == 0), stop=(k == 1))
                    mm.then_inc(S["g_m"], 1)
                for q in range(2):
                    n = i * 2 + q
                    b = bank[2] if q == 0 else bank[7]
                    pe.wait_ge(S["g_ag2"], n + 1 + 2)
                    pe.wait_ge(pair["x2_in"][q], i * 16 + 16)
                    pe.wait_ge(S["g_a2"], n + 1)
                    for k in range(2):
                        pe.transpose(b[:, k * P:(k + 1) * P], tmp_q[:, q, k * P:(k + 1) * P], ident[:, :])
                    for k in range(2):
                        mm = pe.transpose(b[:, (2 + k) * P:(3 + k) * P], hq[:, q, k * P:(k + 1) * P], ident[:, :])
                    mm.then_inc(S["g_t2"], 1)
                for q in range(2):
                    n = i * 2 + q
                    A_b, B_b = bank[3 + 2 * q], bank[4 + 2 * q]
                    pe.wait_ge(S["g_a2"], n + 1 + 2)
                    pe.wait_ge(S["g_tanh"], n + 1)
                    for k in range(2):
                        pe.matmul(A_b[:, :], turned[:, q, k * P:(k + 1) * P], wih[:, k, 0:2 * D], start=(k == 0), stop=False)
                        pe.matmul(A_b[:, :], turned[:, q, (2 + k) * P:(3 + k) * P], whh[:, k, 0:2 * D], start=False, stop=False)
                    pe.matmul(A_b[:, :], ones[0:1, :], gru_bias[:, 0:2 * D], start=False, stop=False)
                    pe.matmul(A_b[:, :], ones[0:1, :], gru_bias[:, 3 * D:5 * D], start=False, stop=True)
                    for k in range(2):
                        pe.matmul(B_b[:, 0:D], turned[:, q, k * P:(k + 1) * P], wih[:, k, 2 * D:3 * D], start=(k == 0), stop=False)
                    pe.matmul(B_b[:, 0:D], ones[0:1, :], gru_bias[:, 2 * D:3 * D], start=False, stop=True)
                    for k in range(2):
                        pe.matmul(B_b[:, D:2 * D], turned[:, q, (2 + k) * P:(3 + k) * P], whh[:, k, 2 * D:3 * D], start=(k == 0), stop=False)
                    pe.matmul(B_b[:, D:2 * D], ones[0:1, :], gru_bias[:, 5 * D:6 * D], start=False, stop=True).then_inc(S["g_ab"], 1)

            with pe.Fori(0, PAIRS) as i:
                for q in range(2):
                    n = i * 2 + q + 2 * NBE
                    pe.wait_ge(S["d_staged"], n + 1)
                    pe.wait_ge(S["d_at"], n + 1 + NBE)
                    turn(n, q, staged_x[:, q, :], 4 + q)
                for q in range(2):
                    n = i * 2 + q
                    pe.wait_ge(S["d_at"], n + 1 + 2 + 3 * NBE)
                    pe.wait_ge(S["d_h"], n + 1 + 2 * NBE)
                    for k in range(2):
                        mm = pe.matmul(bank[6 + q][:, 0:D], turned[:, q, k * P:(k + 1) * P], w0[:, k, :], start=(k == 0), stop=(k == 1))
                    mm.then_inc(S["d_m"], 1)
            scatter_pass(3, 2, P)
            scatter_pass(4, 3, P)

        @block.scalar
        def _(act):
            act.sem_inc(S["sg_cp"], 3)
            for n in ("seg_cp", "d_at", "d_h", "d_h7", "l2_cp", "g_a1", "g_a2", "g_tanh"):
                act.sem_inc(S[n], 2)
            for m, (_, k, o) in enumerate(TURN):
                act.wait_ge(S["wt_turned"], m + 1)
                act.activation(w_tr[:, k, o:o + P], bank[4 + m % 4][:, 0:P], ACT.Copy).then_inc(S["wt_copied"], 1)

            def copy_windows(dests, fills):
                for dst in dests:
                    for lo in range(0, TG, 4):
                        n = min(4, TG - lo) * P
                        act.wait_ge(S["win_turned"], fills + 1)
                        act.activation(dst[:, lo * P:lo * P + n], bank[4 + fills % 4][:, 0:n], ACT.Copy).then_inc(S["wt_copied"], 1)
                        fills += 1
                return fills

            def copy_sums(k):
                with act.Fori(0, T // 8) as i:
                    for h in range(2):
                        act.wait_ge(S["seg_mm"], i * 8 + T * k + 4 * h + 4 + 8)
                        act.activation(tile_sums[:, ds(i * 8 + 4 * h, 4), :].rearrange("p t w -> p (t w)"),
                                       bank[2 + h][:, 0:16], ACT.Copy).then_inc(S["seg_cp"], 1)

            def copy_combine(k):
                for h in range(2):
                    n = (4 if h == 0 else TG - 4) * P
                    act.wait_ge(S["comb_t"], 2 * k + h + 1)
                    act.activation(val_a[:, h * 4 * P:h * 4 * P + n], bank[4 + h][:, 0:n], ACT.Copy).then_inc(S["comb_c"], 1)

            def copy_turned(k):
                with act.Fori(0, TURNS) as i:
                    for g in range(GROUPS):
                        m = i * GROUPS + T // GROUP * k + g
                        act.wait_ge(S["sg_t"], m + 1 + 3)
                        act.wait_ge(S["sg_mm"], m + 1)
                        act.activation(oht[:, g % 3, :], bank[SG_T[g % 3]][:, 0:256].bitcast(BF16), ACT.Copy).then_inc(S["sg_cp"], 1)

            sqrts = [0]

            def square_root(x):
                sqrts[0] += 1
                act.wait_ge(S["sqrt_in"], sqrts[0])
                act.activation(x, x, ACT.Sqrt).then_inc(S["sqrt_out"], 1)

            fills = copy_windows((d_idx, d_loc, d_norm), 0)
            copy_sums(0)
            copy_combine(0)
            copy_combine(1)
            copy_turned(0)
            copy_turned(1)
            square_root(val_a[:, 0:T])
            fills = copy_windows((s_loc, s_idx), fills)

            def copy_block(n, q):
                act.wait_ge(S["d_t"], n + 1 + 2)
                act.wait_ge(S["d_m"], n + 1)
                act.activation(turned[:, q, 0:D], bank[4 + q][:, 0:D], ACT.Copy).then_inc(S["d_at"], 1)

            def d1(i, first):
                for q in range(2):
                    copy_block(i * 2 + q, q)
                for q in range(2):
                    act.wait_ge(S["d_m"], i * 2 + q + 1 + 2)
                    if not first:
                        act.wait_ge(pair["h_out"][q], i * 16)
                    act.activation(hq[:, q, :], bank[6 + q][:, 0:D], ACT.Relu).then_inc(S["d_h"], 1)

            d1(0, True)
            with act.Fori(1, PAIRS) as i:
                d1(i, False)
            with act.Fori(0, PAIRS) as i:
                for q in range(2):
                    copy_block(i * 2 + q + NBE, q)
                for q in range(2):
                    n = i * 2 + q
                    act.wait_ge(S["d_m"], n + NBE + 1 + 2)
                    act.wait_ge(S["d_m2"], n + 1)
                    act.activation(h7t[:, q, 0:P], bank[6 + q][:, 0:P], ACT.Relu, bias=cols[:, 0:1])
                    act.activation(h7t[:, q, P:D], bank[6 + q][:, P:D], ACT.Relu, bias=cols[:, 1:2]).then_inc(S["d_h7"], 1)
            square_root(sm["rstd"][:, 0:NBE])
            square_root(sm["t_a"][:, 0:NBE])
            act.wait_ge(S["gate_step"], 1)
            act.wait_ge(S["pe_chain"], 1)
            act.activation(cols[:, 4:6], bank[1][:, 0:2], ACT.Copy).then_inc(S["gate_step"], 1)
            act.wait_ge(S["pe_chain"], 2)
            act.activation(cols[:, 6:7], bank[1][:, 4:5], ACT.Relu, bias=cols[:, 2:3]).then_inc(S["gate_step"], 1)
            act.wait_ge(S["pe_chain"], 3)
            act.activation(staged_x[0:1, 1, :], bank[1][0:1, 128:128 + D], ACT.Sigmoid).then_inc(S["gate_step"], 1)
            copy_turned(2)
            copy_sums(1)
            copy_combine(2)
            act.wait_ge(S["spa_in"], 1)
            act.activation(sm["spa"][:, 0:NB], sm["spa"][:, 0:NB], ACT.Sigmoid, bias=cols[:, 3:4]).then_inc(S["spa_out"], 1)
            square_root(sm["rstd"][:, 0:NBE])

            def d4(i, first):
                for q in range(2):
                    copy_block(i * 2 + q + 2 * NBE, q)
                for q in range(2):
                    n = i * 2 + q
                    act.wait_ge(S["d_m"], n + 2 * NBE + 1 + 2)
                    if not first:
                        act.wait_ge(pair["tab_out"][q], i * 16)
                    act.activation(hq[:, q, :], bank[2 + q][:, 0:D], ACT.Copy).then_inc(S["d_h"], 1)

            d4(0, True)
            with act.Fori(1, PAIRS) as i:
                d4(i, False)

            def l2_functions(i, first, last):
                for g in range(1 if last else GROUPS):
                    if not last:
                        act.wait_ge(S["l2_t"], i * GROUPS + g + 1)
                        act.wait_ge(S["l2_p"], i * (SPAN // 2) + 2 * g + 2)
                        act.activation(oht[:, g % 2, :], bank[g % 2][:, :], ACT.Copy).then_inc(S["l2_cp"], 1)
                    if runs(g, 1, first, last):
                        for t in range(4 * (g - 1), 4 * g, 2):
                            act.wait_ge(S["l2_add"], i * (SPAN // 2) + t // 2 + 1 + 4)
                            both = msg[:, t % RING:t % RING + 2, 0:D]
                            act.activation(both, both, ACT.Silu).then_inc(S["l2_silu"], 1)

            in_turns(act, TURNS, l2_functions, 1)

            with act.Fori(0, PAIRS) as i:
                for q in range(2):
                    n = i * 2 + q
                    act.wait_ge(S["g_t1"], n + 1 + 2)
                    act.wait_ge(S["g_m"], n + 1)
                    act.activation(h7t[:, q, :], bank[q][:, 0:D], ACT.Copy).then_inc(S["g_a1"], 1)
                for q in range(2):
                    n = i * 2 + q
                    act.wait_ge(S["g_t2"], n + 1 + 2)
                    act.wait_ge(S["g_ab"], n + 1)
                    act.activation(turned[:, q, :], (bank[2] if q == 0 else bank[7])[:, :], ACT.Copy).then_inc(S["g_a2"], 1)
                for q in range(2):
                    n = i * 2 + q
                    act.wait_ge(S["g_ab"], n + 1 + 2)
                    act.wait_ge(S["g_xn"], n + 1)
                    act.activation(rz[:, q, :], bank[3 + 2 * q][:, :], ACT.Sigmoid).then_inc(S["g_rz"], 1)
                for q in range(2):
                    act.wait_ge(S["g_n"], i * 2 + q + 1)
                    act.activation(n_sb[:, q, :], n_sb[:, q, :], ACT.Tanh).then_inc(S["g_tanh"], 1)
            square_root(sm["rstd"][:, 0:NBE])
            square_root(sm["rstd"][:, 0:NBE])
            square_root(sm["t_a"][:, 0:NBE])
            with act.Fori(0, PAIRS) as i:
                for q in range(2):
                    copy_block(i * 2 + q + 3 * NBE, q)
            square_root(sm["rstd"][:, 0:NBE])

        @block.vector
        def _(dve):
            chain = Chain(dve, S["dve_chain"])
            link = chain.link
            regs = [dve.alloc_register(f"dve_blk{j}") for j in range(8)]
            dve.sem_inc(S["accd"], 4)
            dve.sem_inc(S["l2_add"], 4)
            dve.sem_inc(S["l2_acc"], 4)
            dve.sem_inc(S["sg_sel"], 3)
            for n in ("d_res", "p_split", "g_ag2", "g_xn", "f_res", "f_out"):
                dve.sem_inc(S[n], 2)

            dve.memset(src_i, -1).then_inc(S["pads_set"], 1)
            dve.memset(dst_i, -1).then_inc(S["pads_set"], 1)
            dve.memset(w_nat_e, 0.0).then_inc(S["pads_set"], 1)
            dve.memset(dst_next, 1 << 20).then_inc(S["pads_set"], 1)
            dve.memset(zeros[:, :], 0.0)
            dve.memset(x_sb[:, NB - 1:NBE, :], 0.0)
            dve.memset(pay[:, 0:J, 3:4], 0.0)
            dve.memset(pay[:, J:J + RING, :], 0.0)
            dve.wait_ge(S["consts"], 9)
            dve.tensor_copy(ident_b[:, :], ident[:, :])
            dve.tensor_copy(iota[:, :], iota_i[:, :])
            dve.tensor_copy(iota_b[:, :], iota_i[:, :])
            dve.tensor_copy(tile_no[:, :], tile_no_i[:, :])
            link(dve.tensor_scalar(node_real[:, :], node_i[:, :], float(N), None, ALU.is_lt))
            dve.wait_ge(S["edges_in"], 16 * 12)
            dve.tensor_copy(pay[:, 0:J, 0:1].rearrange("p j a -> p (j a)"), src_i[:, 0:J])
            dve.tensor_copy(pay[:, 0:J, 1:2].rearrange("p j a -> p (j a)"), dst_i[:, 0:J])
            dve.tensor_copy(pay[:, 0:J, 2:3].rearrange("p j a -> p (j a)"), w_nat_e)
            dve.tensor_tensor(pos_f, dst_i[:, 0:J], dst_next[:, 0:J], ALU.is_gt)
            link(dve.tensor_scalar(scan_out.bitcast(I32), src_i[:, 0:J], P - 1, None, ALU.bitwise_and))
            link(dve.tensor_copy(src_loc, scan_out.bitcast(I32)))
            dve.tensor_reduce(viol[:, :], pos_f, AX_X, ALU.add)
            link(dve.tensor_scalar(scan_out.bitcast(I32), src_i[:, 0:J], 7, None, ALU.arith_shift_right))
            dve.tensor_copy(src_blk, scan_out.bitcast(I32))
            link(dve.tensor_copy(src_kb, scan_out.bitcast(I32)))
            link(dve.tensor_scalar(scan_out.bitcast(I32), dst_i[:, 0:J], 7, None, ALU.arith_shift_right))
            link(dve.tensor_copy(dst_kb, scan_out.bitcast(I32)))
            with dve.Fori(0, NB) as b:
                chain.enter(b, 2)
                link(dve.tensor_scalar(pos_f, dst_kb, iota[:, ds(b, 1)], 0.0, ALU.is_equal, ALU.add, accum_out=sm["tot_d"][:, ds(b, 1)]))
                link(dve.tensor_scalar(scan_out, src_kb, iota[:, ds(b, 1)], 0.0, ALU.is_equal, ALU.add, accum_out=sm["tot_s"][:, ds(b, 1)]))
            chain.leave(NB)
            dve.sem_inc(S["totals_ready"], 1)
            dve.wait_ge(S["prefix_done"], 1)
            link(dve.tensor_copy(flag_i[:, :], bank[1][:, 128:129]))
            dve.sem_inc(S["flag_ready"], 1)

            def plan_tiles(k, base, win_i):
                c = {n: sm[n][:, 0:NB] for n in ("incl", "off", "t_a", "t_b", "t_incl", "delta", "ge")}
                ia, ib = sm_i["ti_a"][:, 0:NB], sm_i["ti_b"][:, 0:NB]
                total = bank[k][:, 64:64 + NB]
                link(dve.tensor_copy(c["t_a"], total))
                link(dve.tensor_tensor_scan(c["incl"], c["t_a"], c["t_a"], 0.0, ALU.add, ALU.bypass))
                link(dve.tensor_tensor(c["off"], c["incl"], c["t_a"], ALU.subtract))
                link(dve.scalar_tensor_tensor(base[:, 0:NB], c["off"], -1.0, bank[k][:, 0:NB], ALU.add, ALU.add))
                link(dve.tensor_copy(ia, c["off"]))
                link(dve.tensor_scalar(ib, ia, 4, None, ALU.arith_shift_right))
                link(dve.tensor_copy(c["t_b"], ib))
                link(dve.scalar_tensor_tensor(c["t_a"], c["t_b"], -float(CHUNK), c["incl"], ALU.mult, ALU.add))
                link(dve.tensor_scalar(c["t_a"], c["t_a"], float(P - 1), None, ALU.add))
                link(dve.tensor_copy(ia, c["t_a"]))
                link(dve.tensor_scalar(ib, ia, 7, None, ALU.arith_shift_right))
                link(dve.tensor_copy(c["t_a"], ib))
                link(dve.tensor_tensor_scan(c["t_incl"], c["t_a"], c["t_a"], 0.0, ALU.add, ALU.bypass))
                link(dve.tensor_tensor(c["t_a"], c["t_incl"], c["t_a"], ALU.subtract))
                link(dve.scalar_tensor_tensor(c["t_b"], c["t_a"], -float(P // CHUNK), c["t_b"], ALU.mult, ALU.add))
                link(dve.memset(sm["delta"][:, NB - 1:NB], float(2 * NROW)))
                link(dve.tensor_tensor(sm["delta"][:, 0:NB - 1], sm["t_b"][:, 1:NB], sm["t_b"][:, 0:NB - 1], ALU.subtract))
                for g in range(TG):
                    t = tile_no[:, g:g + 1]
                    link(dve.tensor_scalar(c["ge"], c["t_incl"], t, None, ALU.is_le))
                    link(dve.tensor_reduce(ge_sum[:, g:g + 1], c["ge"], AX_X, ALU.add))
                    link(dve.tensor_tensor(c["ge"], c["ge"], c["delta"], ALU.mult))
                    link(dve.tensor_reduce(row_b[:, g:g + 1], c["ge"], AX_X, ALU.add))
                link(dve.tensor_scalar(blk_c[:, :], ge_sum[:, :], float(NB - 1), None, ALU.min))
                link(dve.tensor_scalar(row_b[:, :], row_b[:, :], sm["t_b"][:, 0:1], None, ALU.add))
                link(dve.scalar_tensor_tensor(row_b[:, :], tile_no[:, :], float(P // CHUNK), row_b[:, :], ALU.mult, ALU.add))
                for g in range(TG):
                    link(dve.tensor_scalar(win_i[:, g, :], iota[:, 0:P // CHUNK], row_b[:, g:g + 1], float(NROW - 1), ALU.add, ALU.min))

            def place_blocks(k, blk):
                for g in range(TG):
                    if g >= 2 or k:
                        dve.wait_ge(S["blk_bcast"], k * TG + g - 1)
                    dve.tensor_scalar(diag[:, g % 2, :], ident[:, :], blk_c[:, g:g + 1], None, ALU.mult).then_inc(S["diag_ready"], 1)
                dve.wait_ge(S["blk_bcast"], (k + 1) * TG)
                dve.tensor_copy(blk[:, 0:512], bank[2][:, :])
                link(dve.tensor_copy(blk[:, 512:TC], bank[3][:, 0:TC - 512]))

            plan_tiles(0, sm["base_d"], win_i_d)
            dve.sem_inc(S["win_d_ready"], 1)
            for g in range(TG):
                link(dve.tensor_scalar(tile_oh[:, g, :], iota[:, 0:NB], blk_c[:, g:g + 1], None, ALU.is_equal))
            place_blocks(0, blk_d)
            plan_tiles(1, sm["base_s"], win_i_s)
            dve.sem_inc(S["win_s_ready"], 1)
            place_blocks(1, blk_s)

            def positions(kb, base, pos):
                link(dve.tensor_copy(pos_f, pos_start[:, :]))
                with dve.Fori(0, NB) as b:
                    chain.enter(b, 3)
                    link(dve.tensor_scalar(mask, kb, iota[:, ds(b, 1)], None, ALU.is_equal))
                    link(dve.tensor_tensor_scan(scan_out, mask, mask, base[:, ds(b, 1)], ALU.add, ALU.bypass))
                    apart(dve, S["waited"])
                    link(dve.copy_predicated(pos_f, mask.bitcast(I16), scan_out))
                chain.leave(NB)
                link(dve.tensor_copy(pos[:, 0:J], pos_f))

            link(dve.memset(pos_s[:, J:J + RING], 0))
            positions(src_kb, sm["base_s"], pos_s)
            dve.sem_inc(S["pos_s_ready"], 1)
            unsorted = dve.value_load(flag_i[0:1, 0:1], min_val=0, max_val=E)
            link(dve.memset(stats[:, 0, 0:1], 0.0))
            with dve.If(unsorted > 0):
                positions(dst_kb, sm["base_d"], pos_d)
                dve.sem_inc(S["slow_pos"], 1)
            with dve.Else():
                dve.sem_inc(S["dve_chain"], 3 * NB + 2)

            dve.wait_ge(S["wt_copied"], len(TURN) + 6)
            link(dve.tensor_copy(val_a[:, :], blk_d[:, :]))
            link(dve.scalar_tensor_tensor(d_loc[:, :], val_a, -float(P), d_loc[:, :], ALU.mult, ALU.add))
            link(dve.tensor_copy(val_b.bitcast(I32), d_idx[:, :]))
            link(dve.tensor_scalar(val_a.bitcast(I32), val_b.bitcast(I32), P - 1, None, ALU.bitwise_and))
            link(dve.tensor_copy(d_sloc, val_a.bitcast(I32)))
            link(dve.tensor_scalar(val_a.bitcast(I32), val_b.bitcast(I32), 7, None, ALU.arith_shift_right))
            link(dve.tensor_copy(d_sblk, val_a.bitcast(I32)))
            link(dve.tensor_scalar(d_idx[:, :], d_idx[:, :], 0.0, None, ALU.max))

            def split3(dst, src, rest):
                link(dve.tensor_copy(dst(0), src))
                link(dve.tensor_tensor(rest, src, dst(0), ALU.subtract))
                link(dve.tensor_copy(dst(1), rest))
                link(dve.tensor_tensor(dst(2), rest, dst(1), ALU.subtract))

            part_of = lambda s: parts[:, :, s:s + 1].rearrange("p t a -> p (t a)")
            link(dve.memset(part_of(3), 1.0))

            def segment_onehots(k):
                dve.sem_inc(S["seg_ready"], 1)
                with dve.Fori(0, T // 8) as i:
                    for u in range(8):
                        dve.wait_ge(S["seg_mm"], i * 8 + T * k + u + 1)
                        dve.tensor_scalar(ohb[:, u, :], iota_b[:, :], d_loc[:, ds(i * 8 + u, 1)], None, ALU.is_equal).then_inc(S["seg_oh"], 1)
                dve.wait_ge(S["seg_cp"], T // 4 * (k + 1) + 2)

            def combine(k, first, last, dst):
                w = lambda s: tile_sums[:, 0:T, s:s + 1].rearrange("p t a -> p (t a)")
                link(dve.tensor_copy(val_b[:, 0:T], w(first)))
                for s in range(first + 1, last + 1):
                    link(dve.tensor_tensor(val_b[:, 0:T], val_b[:, 0:T], w(s), ALU.add))
                link(dve.memset(val_b[:, T:TC], 0.0))
                dve.sem_inc(S["comb_v"], 1)
                dve.wait_ge(S["comb_done"], k + 1)
                link(dve.tensor_copy(dst[:, 0:NB], bank[1][:, 0:NB]))

            def node_values(k, values, loc, blk, to):
                split3(lambda s: table3[:, s, 0:NB], values[:, 0:NB], sm["t_b"][:, 0:NB])
                dve.sem_inc(S["sg_ready"], 1)

                def turn_of(i, first, last):
                    for g in range(3 if last else GROUPS):
                        m = i * GROUPS + T // GROUP * k + g
                        if not last:
                            dve.wait_ge(S["sg_t"], m + 1)
                            for u in range(GROUP):
                                dve.tensor_scalar(ohb[:, g % 3 * GROUP + u, :], iota_b[:, :], loc[:, ds(i * SPAN + 4 * g + u, 1)],
                                                  None, ALU.is_equal).then_inc(S["sg_oh"], 1)
                        if runs(g, 3, first, last):
                            dve.wait_ge(S["sg_mm"], m - 3 + 1 + 3)
                            dve.wait_ge(S["sg_sel"], m - 3 + 3)
                            for u in range(GROUP):
                                t = ds(i * SPAN + 4 * (g - 3) + u, 1)
                                sel = dve.scalar_tensor_tensor(junk[:, u, 0:NB], iota[:, 0:NB], blk[:, t],
                                                               bank[SG_S[g % 3]][:, u * 64:u * 64 + NB],
                                                               ALU.is_equal, ALU.mult, accum_out=to[:, t])
                            sel.then_inc(S["sg_sel"], 1)

                in_turns(dve, TURNS, turn_of, 3)
                dve.wait_ge(S["sg_sel"], T // GROUP * (k + 1) + 3)

            split3(part_of, d_norm[:, :], val_a)
            segment_onehots(0)
            combine(0, 0, 2, sm["deg_in"])
            combine(1, 3, 3, sm["cnt_in"])
            with dve.Fori(0, J // 8) as i:
                for u in range(8):
                    dve.wait_ge(S["deg_mm"], i * 8 + u + 1)
                    t = ds(i * 8 + u, 1)
                    dve.tensor_scalar(oh[:, 4 + u % 4, :], iota[:, :], src_loc[:, t], w_nat_e[:, t], ALU.is_equal, ALU.mult)
                    dve.tensor_scalar(junk[:, u % 4, 0:NB], iota[:, 0:NB], src_blk[:, t], None, ALU.is_equal).then_inc(S["deg_oh"], 1)
            dve.wait_ge(S["deg_mm"], J + 4)
            link(dve.tensor_copy(sm["deg_out"][:, 0:NB], bank[0][:, 0:NB]))
            link(dve.tensor_copy(s_idx[:, :], blk_d[:, :]))
            node_values(0, sm["deg_in"], d_loc, s_idx, val_b)
            node_values(1, sm["deg_out"], d_sloc, d_sblk, val_a)
            link(dve.tensor_tensor(val_a[:, 0:T], val_a[:, 0:T], val_b[:, 0:T], ALU.mult))
            link(dve.tensor_scalar(val_a[:, 0:T], val_a[:, 0:T], 1e-12, None, ALU.add))
            dve.sem_inc(S["sqrt_in"], 1)
            dve.wait_ge(S["sqrt_out"], 1)
            link(dve.reciprocal(val_a[:, 0:T], val_a[:, 0:T]))
            link(dve.tensor_tensor(d_norm[:, 0:T], d_norm[:, 0:T], val_a[:, 0:T], ALU.mult))
            dve.sem_inc(S["l0_ready"], 1)
            dve.wait_ge(S["wt_copied"], len(TURN) + 10)
            link(dve.tensor_copy(val_a[:, :], blk_s[:, :]))
            link(dve.scalar_tensor_tensor(s_loc[:, :], val_a, -float(P), s_loc[:, :], ALU.mult, ALU.add))
            link(dve.tensor_scalar(s_idx[:, :], s_idx[:, :], 0.0, None, ALU.max))

            def scatter_pass(k, loc, weight, blk, lo, width):
                with dve.Fori(0, TURNS) as i:
                    def add(u):
                        if u % RING == 0:
                            dve.load(regs, blk[0:1, ds(i * SPAN + u, RING)])
                        n = i * SPAN + T * k + u
                        b = dve.snap(regs[u % RING], min_val=0, max_val=NB - 1)
                        dve.wait_ge(S["mm"], n + 1 + 8)
                        dve.wait_ge(S["accd"], n + 4)
                        to = acc[:, ds(b, 1), lo:lo + width].rearrange("p a f -> p (a f)")
                        dve.tensor_tensor(to, bank[u % 4][:, 0:width], to, ALU.add).then_inc(S["accd"], 1)

                    for u in range(SPAN + 2):
                        if u < SPAN:
                            t = ds(i * SPAN + u, 1)
                            dve.wait_ge(S["mm"], i * SPAN + T * k + u + 5)
                            if weight is None:
                                o = dve.tensor_scalar(oh[:, u % 4, :], iota[:, :], loc[:, t], None, ALU.is_equal)
                            else:
                                o = dve.tensor_scalar(oh[:, u % 4, :], iota[:, :], loc[:, t], weight[:, t], ALU.is_equal, ALU.mult)
                            o.then_inc(S["one_hot"], 1)
                        if u >= 2:
                            add(u - 2)
                dve.wait_ge(S["accd"], T * (k + 1) + 4)

            def stage_block(n, q, base):
                dve.wait_ge(S["d_t"], n + base + 1)
                dve.tensor_scalar(staged_x[:, q, :], acc[:, ds(n, 1), 0:D].rearrange("p a f -> p (a f)"), 1.0, None, ALU.mult).then_inc(S["d_staged"], 1)

            x_of = lambda n: x_sb[:, ds(n, 1), :].rearrange("p a f -> p (a f)")

            def statistics(n, q):
                apart(dve, S["waited"])
                link(dve.bn_stats(stats[:, q, :], x_of(n)))
                apart(dve, S["waited"])
                link(dve.bn_aggr(mv_one[:, q, :], stats[:, q, :]))
                return dve.tensor_scalar(mv[:, ds(n, 1), :].rearrange("p a w -> p (a w)"), mv_one[:, q, :], 1.0, None, ALU.mult)

            sqrts = [1]

            def square_root(x):
                sqrts[0] += 1
                dve.sem_inc(S["sqrt_in"], 1)
                dve.wait_ge(S["sqrt_out"], sqrts[0])
                link(dve.reciprocal(x, x))

            mean, rstd = sm["mean"][:, 0:NBE], sm["rstd"][:, 0:NBE]

            def normalizers(masked=False):
                link(dve.tensor_copy(mean, mv[:, :, 0:1].rearrange("p b a -> p (b a)")))
                link(dve.tensor_scalar(rstd, mv[:, :, 1:2].rearrange("p b a -> p (b a)"), 1e-5, None, ALU.add))
                square_root(rstd)
                if masked:
                    link(dve.tensor_tensor(rstd, rstd, node_real[:, :], ALU.mult))

            def normalize(to, n):
                return dve.tensor_scalar(to, x_of(n), mean[:, ds(n, 1)], rstd[:, ds(n, 1)], ALU.subtract, ALU.mult)

            dve.wait_ge(S["wt_stored"], 32)
            link(dve.memset(acc_flat, 0.0))
            scatter_pass(0, d_loc, d_norm, blk_d, 0, D)
            with dve.Fori(0, PAIRS) as i:
                for q in range(2):
                    stage_block(i * 2 + q, q, 0)
            dve.wait_ge(S["d_staged"], NBE)
            link(dve.memset(acc_flat, 0.0))
            scatter_pass(1, d_loc, d_norm, blk_d, 0, D)
            dve.wait_ge(S["x_in"], 32)
            with dve.Fori(0, PAIRS) as i:
                chain.enter(i, 6)
                for q in range(2):
                    stage_block(i * 2 + q, q, NBE)
                for q in range(2):
                    n = i * 2 + q
                    dve.wait_ge(S["d_m2"], n + 1 + 2)
                    link(dve.tensor_tensor(x_of(n), bank[2 + q][:, 0:D], x_of(n), ALU.add))
                    statistics(n, q).then_inc(S["d_res"], 1)
            chain.leave(PAIRS)
            dve.wait_ge(S["d_res"], NBE + 2)
            normalizers(masked=True)
            link(dve.memset(sm["t_a"][:, 0:NBE], 0.0))
            link(dve.tensor_scalar(sm["t_a"][:, 0:NB], sm["cnt_in"][:, 0:NB], 0.0, None, ALU.add))
            link(dve.tensor_scalar(sm["t_a"][:, 0:NBE], sm["t_a"][:, 0:NBE], 1.0, None, ALU.add))
            square_root(sm["t_a"][:, 0:NBE])
            link(dve.tensor_copy(sm["dis"][:, 0:NBE], sm["t_a"][:, 0:NBE]))
            with dve.Fori(0, NBE) as b:
                chain.enter(b, 2)
                link(normalize(x_of(b), b))
                dve.sem_inc(S["col_ready"], 1)
                link(dve.scalar_tensor_tensor(tmp_q[:, 0, :], x_of(b), 1.0, gw_bc[:, :], ALU.mult, ALU.mult, accum_out=sm["h"][:, ds(b, 1)]))
            chain.leave(NBE)
            dve.wait_ge(S["col_done"], NBE)
            link(dve.tensor_scalar(staged_x[0:1, 0, :], bank[0][0:1, 256:256 + D], 1.0 / N, None, ALU.mult))
            dve.sem_inc(S["gate_step"], 1)
            dve.wait_ge(S["pe_chain"], 4)
            link(dve.tensor_scalar(gate_bc[:, :], bank[4][:, 0:D], 2.0, None, ALU.add))
            dve.sem_inc(S["gate_done"], 1)
            link(dve.tensor_tensor(sm["hd"][:, 0:NB], sm["h"][:, 0:NB], sm["dis"][:, 0:NB], ALU.mult))
            node_values(2, sm["hd"], d_sloc, d_sblk, val_a)
            link(dve.memset(val_a[:, T:TC], 0.0))
            split3(part_of, val_a, val_b)
            segment_onehots(1)
            combine(2, 0, 2, sm["spa"])
            link(dve.tensor_tensor(sm["spa"][:, 0:NB], sm["spa"][:, 0:NB], sm["hd"][:, 0:NB], ALU.add))
            link(dve.tensor_tensor(sm["spa"][:, 0:NB], sm["spa"][:, 0:NB], sm["dis"][:, 0:NB], ALU.mult))
            link(dve.memset(sm["spa"][:, NB:NBE], 0.0))
            dve.sem_inc(S["spa_in"], 1)
            dve.wait_ge(S["spa_out"], 1)
            with dve.Fori(0, NBE) as b:
                chain.enter(b, 4)
                link(dve.scalar_tensor_tensor(x_of(b), gate_bc[:, :], sm["spa"][:, ds(b, 1)], x_of(b), ALU.add, ALU.mult))
                link(statistics(b, 0))
            chain.leave(NBE)
            normalizers()
            with dve.Fori(0, NBE) as b:
                chain.enter(b, 1)
                link(normalize(x_of(b), b))
            chain.leave(NBE)
            dve.sem_inc(S["x2_done"], 1)
            dve.wait_ge(S["p_loaded"], 16)
            link(dve.memset(acc_flat, 0.0))
            with dve.Fori(0, PAIRS) as i:
                chain.enter(i, 6)
                for q in range(2):
                    n = i * 2 + q
                    dve.wait_ge(S["d_m"], n + 2 * NBE + 1 + 2)
                    s3 = lambda s: p3[:, s, ds(n, 1), :].rearrange("p a f -> p (a f)")
                    P_b = bank[6 + q][:, 0:D]
                    link(dve.tensor_copy(s3(0), P_b))
                    link(dve.tensor_tensor(tmp_q[:, q, :], P_b, s3(0), ALU.subtract))
                    link(dve.tensor_copy(s3(1), tmp_q[:, q, :]))
                    dve.tensor_tensor(s3(2), tmp_q[:, q, :], s3(1), ALU.subtract).then_inc(S["p_split"], 1)
            chain.leave(PAIRS)
            dve.wait_ge(S["p_split"], NBE + 2)
            link(dve.memset(msg[:, :, D:D + 1], 1.0))
            dve.sem_inc(S["pass_ready"], 1)

            def l2_sums(i, first, last):
                for g in range(3 if last else GROUPS):
                    if not last:
                        dve.wait_ge(S["l2_c"], i * SPAN + 4 * g + 4)
                        for u in range(GROUP):
                            t = 4 * g + u
                            dve.tensor_scalar(oh[:, t % 12, :], iota[:, :], s_loc[:, ds(i * SPAN + t, 1)], None, ALU.is_equal).then_inc(S["l2_oh"], 1)
                    if runs(g, 3, first, last):
                        for u in range(GROUP):
                            t = 4 * (g - 3) + u
                            if t % RING == 0:
                                dve.load(regs, blk_s[0:1, ds(i * SPAN + t, RING)])
                            b = dve.snap(regs[t % RING], min_val=0, max_val=NB - 1)
                            dve.wait_ge(S["l2_c"], i * SPAN + t + 1 + 12)
                            dve.wait_ge(S["l2_acc"], i * SPAN + t + 4)
                            to = acc[:, ds(b, 1), :].rearrange("p a f -> p (a f)")
                            dve.tensor_tensor(to, bank[4 + u][:, 0:D + 1], to, ALU.add).then_inc(S["l2_acc"], 1)
                    if runs(g, 1, first, last):
                        for t in range(4 * (g - 1), 4 * g, 2):
                            dve.wait_ge(S["l2_p"], i * (SPAN // 2) + t // 2 + 1 + 4)
                            for w in range(t, t + 2):
                                dve.wait_ge(gd[w % RING], i * 48 + 16 * (T // RING * 2 + w // RING + 1))
                            dve.wait_ge(S["l2_c"], i * SPAN + t + 6)
                            both = slice(t % RING, t % RING + 2)
                            dve.tensor_tensor(msg[:, both, 0:D], bank[2 + t // 2 % 2][:, :].rearrange("p (r f) -> p r f", r=2),
                                              gbuf[:, both, 0:D], ALU.add).then_inc(S["l2_add"], 1)

            in_turns(dve, TURNS, l2_sums, 3)
            dve.wait_ge(S["l2_acc"], T + 4)
            dve.sem_inc(S["g_done"], 1)
            dve.wait_ge(S["w5_in"], 16 * 9)
            with dve.Fori(0, PAIRS) as i:
                chain.enter(i, 18)
                for q in range(2):
                    n = i * 2 + q
                    cnt = acc[:, ds(n, 1), D:D + 1].rearrange("p a f -> p (a f)")
                    dve.wait_ge(S["g_t1"], n + 1)
                    link(dve.tensor_scalar(cnt_c[:, q, 0:1], cnt, 1e-8, None, ALU.add))
                    link(dve.reciprocal(cnt_c[:, q, 0:1], cnt_c[:, q, 0:1]))
                    link(dve.tensor_tensor(cnt_c[:, q, 1:2], cnt, cnt_c[:, q, 0:1], ALU.mult))
                    dve.tensor_scalar(staged_x[:, q, :], acc[:, ds(n, 1), 0:D].rearrange("p a f -> p (a f)"), cnt_c[:, q, 0:1],
                                      None, ALU.mult).then_inc(S["g_agg"], 1)
                for q in range(2):
                    n = i * 2 + q
                    dve.wait_ge(S["g_m"], n + 1 + 2)
                    dve.wait_ge(S["g_t2"], n + 1)
                    dve.scalar_tensor_tensor(tmp_q[:, q, :], b2_bc, cnt_c[:, q, 1:2], bank[q][:, D:2 * D],
                                             ALU.mult, ALU.add).then_inc(S["g_ag2"], 1)
                for q in range(2):
                    n = i * 2 + q
                    dve.wait_ge(S["g_rz"], n + 1)
                    link(dve.tensor_tensor(n_sb[:, q, :], bank[4 + 2 * q][:, D:2 * D], rz[:, q, 0:D], ALU.mult))
                    dve.tensor_tensor(n_sb[:, q, :], bank[4 + 2 * q][:, 0:D], n_sb[:, q, :], ALU.add).then_inc(S["g_n"], 1)
                for q in range(2):
                    n = i * 2 + q
                    dve.wait_ge(S["g_tanh"], n + 1 + 2)
                    dve.wait_ge(pair["x2_in"][q], i * 16 + 16)
                    link(dve.tensor_tensor(hq[:, q, :], hq[:, q, :], n_sb[:, q, :], ALU.subtract))
                    link(dve.tensor_tensor(hq[:, q, :], hq[:, q, :], rz[:, q, D:2 * D], ALU.mult))
                    link(dve.tensor_tensor(x_of(n), hq[:, q, :], n_sb[:, q, :], ALU.add))
                    statistics(n, q).then_inc(S["g_xn"], 1)
            chain.leave(PAIRS)
            dve.wait_ge(S["g_xn"], NBE + 2)
            normalizers()
            with dve.Fori(0, PAIRS) as i:
                chain.enter(i, 12)
                for q in range(2):
                    n = i * 2 + q
                    dve.wait_ge(pair["x2b_in"][q], i * 16 + 16)
                    link(dve.tensor_tensor(hq[:, q, :], hq[:, q, :], beta_bc, ALU.add))
                    link(normalize(x_of(n), n))
                    link(dve.tensor_tensor(x_of(n), x_of(n), gamma_bc, ALU.mult))
                    link(dve.tensor_tensor(x_of(n), x_of(n), hq[:, q, :], ALU.add))
                    statistics(n, q).then_inc(S["f_res"], 1)
            chain.leave(PAIRS)
            dve.wait_ge(S["f_res"], NBE + 2)
            normalizers()
            link(dve.tensor_scalar(sm["t_a"][:, 0:NBE], acc[:, :, D:D + 1].rearrange("p b a -> p (b a)"), 1.0, None, ALU.add))
            square_root(sm["t_a"][:, 0:NBE])
            link(dve.tensor_copy(sm["ri"][:, 0:NBE], sm["t_a"][:, 0:NBE]))
            link(dve.memset(acc_flat, 0.0))
            scales = (sm["dis"], sm["ri"])
            def d6(i, first):
                chain.enter(i, 2)
                for q in range(2):
                    n = i * 2 + q
                    link(normalize(x_of(n), n))
                    dve.wait_ge(S["d_t"], n + 3 * NBE + 1)
                    dve.tensor_scalar(staged_x[:, q, :], x_of(n), 1.0, None, ALU.mult).then_inc(S["d_staged"], 1)
                for q in range(2):
                    n = i * 2 + q
                    dve.wait_ge(S["d_m"], n + 3 * NBE + 1 + 2)
                    dve.wait_ge(pair["tab_out"][q], i * 32 + 16 * PAIRS)
                    dve.tensor_scalar(hq[:, q, 0:P], bank[6 + q][:, 0:P], scales[0][:, ds(n, 1)], None, ALU.mult)
                    dve.tensor_scalar(hq[:, q, P:D], bank[6 + q][:, P:D], scales[1][:, ds(n, 1)], None, ALU.mult).then_inc(S["d_h"], 1)
            with dve.Fori(0, PAIRS) as i:
                d6(i, False)
            chain.leave(PAIRS)
            scatter_pass(2, s_loc, None, blk_s, 0, P)
            scatter_pass(3, d_loc, None, blk_d, P, P)
            dve.sem_inc(S["final_ready"], 1)
            with dve.Fori(0, PAIRS) as i:
                chain.enter(i, 12)
                for q in range(2):
                    n = i * 2 + q
                    dve.wait_ge(pair["fin_in"][q], i * 32 + 32)
                    link(dve.tensor_tensor(tmp_q[:, q, :], acc[:, ds(n, 1), 0:D].rearrange("p a f -> p (a f)"), hq[:, q, :], ALU.add))
                    dve.scalar_tensor_tensor(tmp_q[:, q, 0:P], tmp_q[:, q, 0:P], sm["ri"][:, ds(n, 1)], bias_bc[:, 0:P], ALU.mult, ALU.add)
                    link(dve.scalar_tensor_tensor(tmp_q[:, q, P:D], tmp_q[:, q, P:D], sm["dis"][:, ds(n, 1)], bias_bc[:, P:D], ALU.mult, ALU.add))
                    link(dve.tensor_tensor(x_of(n), x_of(n), tmp_q[:, q, :], ALU.add))
                    link(statistics(n, q))
                    dve.sem_inc(S["f_out"], 1)
            chain.leave(PAIRS)
            normalizers()

            def last_norm(i, first):
                for q in range(2):
                    if not first:
                        dve.wait_ge(pair["y_out"][q], i * 16)
                    normalize(staged_x[:, q, :], i * 2 + q).then_inc(S["y_ready"], 1)

            last_norm(0, True)
            with dve.Fori(1, PAIRS) as i:
                last_norm(i, False)


INPUTS = ["x", "src", "dst", "edge_weight", "L0_gnn_W6", "L0_gnn_b6", "L0_gnn_W7", "L0_gnn_b7", "L0_gnn_Wp", "L0_gnn_bp",
          "L1_gnn_w1", "L1_gnn_b1", "L1_gnn_w2", "L1_gnn_b2", "L1_gnn_gcn_w", "L1_gnn_gcn_b", "L2_gnn_W1", "L2_gnn_b1",
          "L2_gnn_W2", "L2_gnn_b2", "L2_gnn_w_ih", "L2_gnn_w_hh", "L2_gnn_b_ih", "L2_gnn_b_hh", "L2_gnn_gamma", "L2_gnn_beta",
          "L3_gnn_W_f", "L3_gnn_W_b", "L3_gnn_bias_param"]


def kernel(**inputs):
    import numpy as np
    import concourse.bacc as bacc
    from concourse.bass_utils import run_bass_kernel_spmd

    nc = bacc.Bacc("TRN2", target_bir_lowering=False, num_devices=1)
    arrays, aps = {}, {}
    for name in INPUTS:
        a = np.ascontiguousarray(inputs[name])
        arrays[f"in_{name}"] = a
        aps[name] = nc.dram_tensor(f"in_{name}", a.shape, mybir.dt.from_np(a.dtype), kind="ExternalInput").ap()
    out = nc.dram_tensor("out_0", inputs["x"].shape, F32, kind="ExternalOutput").ap()
    build(nc, aps, out)
    return run_bass_kernel_spmd(nc, [arrays], core_ids=[0]).results[0]["out_0"]
```

```python
from contextlib import ExitStack

import concourse.bass as bass
from concourse import mybir

ALU = mybir.AluOpType
ACT = mybir.ActivationFunctionType
AX_X = mybir.AxisListType.X
F32 = mybir.dt.float32
BF16 = mybir.dt.bfloat16
I32 = mybir.dt.int32
I16 = mybir.dt.int16
ds = bass.ds

P = 128
D = 256
GROUP = 4
RING = 8
SPAN = 24
CHUNK = 16
WORDS = 4


def apart(engine, sem):
    engine.sem_inc(sem, 1)


def in_turns(engine, turns, turn, lag):
    turn(0, True, False)
    with engine.Fori(1, turns) as i:
        turn(i, False, False)
    if lag:
        turn(turns, False, True)


def runs(g, lag, first, last):
    return g >= lag if first else g < lag if last else True


class Chain:

    def __init__(self, engine, sem):
        self.engine, self.sem, self.count, self.start = engine, sem, 0, None

    def link(self, instruction):
        instruction.then_inc(self.sem, 1)
        self.count += 1
        base = 0 if self.start is None else self.start
        self.engine.wait_ge(self.sem, base + self.count)

    def enter(self, turn, per_turn):
        self.before, self.per_turn = self.count, per_turn
        self.start, self.count = turn * per_turn + self.before, 0

    def leave(self, turns):
        assert self.count == self.per_turn, (self.count, self.per_turn)
        self.start, self.count = None, self.before + turns * self.per_turn


def build(nc, A, out):
    N, _ = A["x"].shape
    E = A["src"].shape[0]
    NB = -(-N // P)
    NBE = NB + NB % 2
    PAIRS = NBE // 2
    LAST = N - (NB - 1) * P
    J = -(-E // (P * SPAN)) * SPAN
    FULL = E // J
    TAIL = E - FULL * J
    T_MAX = (E + NB * (P - 1 + CHUNK - 1)) // P
    T = -(-T_MAX // SPAN) * SPAN
    TURNS = T // SPAN
    TG = -(-T // P)
    TC = TG * P
    GROUPS = SPAN // GROUP
    NROW = P * J // CHUNK
    ROW_PAD = NROW - P // CHUNK - 1
    assert ROW_PAD * CHUNK >= E and TAIL > 1

    rec_d = nc.dram_tensor("records_by_dst", [P * J, WORDS], F32).ap()
    rec_s = nc.dram_tensor("records_by_src", [P * J, WORDS], F32).ap()
    wt_dram = nc.dram_tensor("weights_transposed", [2, P, 2560], F32).ap()
    h6_dram = nc.dram_tensor("h6_table", [NBE * P, D], F32).ap()
    q_dram = nc.dram_tensor("q_table", [NBE * P, D], F32).ap()
    x2_dram = nc.dram_tensor("x2_table", [NBE * P, D], F32).ap()
    fwd_dram = nc.dram_tensor("fwd_table", [NBE * P, P], F32).ap()
    bwd_dram = nc.dram_tensor("bwd_table", [NBE * P, P], F32).ap()

    ctx = ExitStack()
    with ctx:
        def sb(name, shape, dt=F32):
            return ctx.enter_context(nc.sbuf_tensor(name, shape, dt))

        def sem(name):
            return ctx.enter_context(nc.semaphore(name))

        bank = [ctx.enter_context(nc.psum_tensor(f"bank{i}", [P, 512], F32)) for i in range(8)]

        NX = NBE * D
        big = sb("big", [P, 3 * NBE * D // 2])
        x_sb = big[:, 0:NX].rearrange("p (b f) -> p b f", f=D)
        p3 = big[:, :].bitcast(BF16).rearrange("p (s b f) -> p s b f", s=3, f=D)
        SP0 = NX
        spare = lambda a, n: big[:, SP0 + a:SP0 + a + n]
        d_sloc, d_sblk = spare(0, TC), spare(TC, TC)
        val_a, val_b = spare(2 * TC, TC), spare(3 * TC, TC)
        pos_start = spare(2 * TC, J).bitcast(I32)
        parts = spare(4 * TC, 2 * TC).bitcast(BF16).rearrange("p (t w) -> p t w", w=4)
        wih = spare(0, 1536).rearrange("p (k n) -> p k n", k=2)
        whh = spare(1536, 1536).rearrange("p (k n) -> p k n", k=2)
        w2t = spare(3072, 512).rearrange("p (k n) -> p k n", k=2)
        b2_bc, gamma_bc, beta_bc = (spare(3584 + D * k, D) for k in range(3))

        acc = sb("acc", [P, NBE, D + 1])
        acc_flat = acc[:, :, :].rearrange("p b f -> p (b f)")
        w_nat = acc_flat[:, 0:5120]
        w_tr = acc_flat[:, 5120:10240].rearrange("p (k n) -> p k n", k=2)
        win_s = acc_flat[:, 0:TG * 512].rearrange("p (g s w) -> p g s w", g=TG, w=WORDS)

        ring = sb("ring", [P, 2 * RING * (D + 1)])
        gbuf = ring[:, 0:RING * (D + 1)].rearrange("p (r f) -> p r f", f=D + 1)
        msg = ring[:, RING * (D + 1):].rearrange("p (r f) -> p r f", f=D + 1)
        win_d = ring[:, 0:TG * 512].rearrange("p (g s w) -> p g s w", g=TG, w=WORDS)
        tile_sums = ring[:, 0:TC * 4].rearrange("p (t w) -> p t w", w=4)
        gru_bias = ring[0:3, 0:6 * D]
        rest_rows, part_rows = ring[0:3, 6 * D:8 * D], ring[0:3, 10 * D + 8:11 * D + 8].bitcast(BF16)
        h7t = ring[:, 8 * D + 8:10 * D + 8].rearrange("p (q n) -> p q n", q=2)
        tmp_q = ring[:, 2 * RING * (D + 1) - 2 * D:].rearrange("p (q n) -> p q n", q=2)

        at = [0]

        def part(n, dt=F32):
            a = big[:, at[0]:at[0] + n]
            at[0] += n
            return a if dt == F32 else a.bitcast(dt)

        pay = part((J + RING) * WORDS).rearrange("p (j w) -> p j w", w=WORDS)
        src_i, dst_i = part(J + RING, I32), part(J + RING, I32)
        w_nat_e = part(J)
        dst_next = part(J + RING, I32)
        src_kb, dst_kb = part(J // 2, BF16), part(J // 2, BF16)
        src_blk, src_loc = part(J), part(J)
        pos_f, scan_out = part(J), part(J)
        mask = part(J // 2, BF16)
        pos_d = dst_next
        pos_s = src_i
        assert at[0] <= (NB - 1) * D

        d_idx, d_loc, d_norm = sb("d_idx", [P, TC]), sb("d_loc", [P, TC]), sb("d_norm", [P, TC])
        s_idx, s_loc = sb("s_idx", [P, TC]), sb("s_loc", [P, TC])
        blk_d, blk_s = sb("blk_d", [P, TC], I32), sb("blk_s", [P, TC], I32)
        tile_oh = sb("tile_oh", [P, TG, NB])

        oh = sb("oh", [P, 3 * GROUP, P])
        ohb = oh[:, 0:6, :].rearrange("p r n -> p (r n)").bitcast(BF16).rearrange("p (r n) -> p r n", n=P)
        oht = sb("oht", [P, 3, GROUP * P], BF16)
        stage_i = sb("stage_i", [P, 3, RING], I32)
        stage_r = sb("stage_r", [P, 3, RING, WORDS])
        staged_x, turned = sb("staged_x", [P, 2, D]), sb("turned", [P, 2, 512])
        hq = sb("hq", [P, 2, D])
        wbuf = sb("wbuf", [P, 1536])
        gru_rows = wbuf[0:3, 2 * D:5 * D].bitcast(BF16)
        ones_b = sb("ones_b", [3, P], BF16)
        bias_rows = sb("bias_rows", [1, 2 * D])

        ident, ones = sb("ident", [P, P]), sb("ones", [P, P])
        ident_b, iota_b = sb("ident_b", [P, P], BF16), sb("iota_b", [P, P], BF16)
        iota_i, iota = sb("iota_i", [P, P], I32), sb("iota", [P, P])
        before = sb("before", [P, P])
        diag = hq[:, 0, :].rearrange("p (g n) -> p g n", g=2)
        tile_no_i, tile_no = sb("tile_no_i", [P, TG], I32), sb("tile_no", [P, TG])
        node_i, node_real = sb("node_i", [P, NBE], I32), sb("node_real", [P, NBE])
        sm = {n: sb(n, [P, NB + 1]) for n in (
            "tot_d", "tot_s", "incl", "off", "base_d", "base_s", "t_a", "t_b", "t_incl", "delta",
            "deg_out", "deg_in", "cnt_in", "dis", "ri", "hd", "h", "spa", "mean", "rstd", "ge")}
        sm_i = {n: sb(n, [P, NB + 1], I32) for n in ("ti_a", "ti_b")}
        row_b, blk_c, ge_sum = sb("row_b", [P, TG]), sb("blk_c", [P, TG]), sb("ge_sum", [P, TG])
        win_i_d, win_i_s = sb("win_i_d", [P, TG, 8], I32), sb("win_i_s", [P, TG, 8], I32)
        table3 = sb("table3", [P, 3, NB + 1], BF16)
        viol, flag_i = sb("viol", [P, 1]), sb("flag_i", [P, 1], I32)
        stats, mv_one, mv = sb("stats", [P, 2, 6]), sb("mv_one", [P, 2, 2]), sb("mv", [P, NBE, 2])
        cols = sb("cols", [P, 16])
        gw_bc, gate_bc, bias_bc = sb("gw_bc", [P, D]), sb("gate_bc", [P, D]), sb("bias_bc", [P, D])
        junk = sb("junk", [P, 8, NBE])
        zeros = gate_bc
        SG_T, SG_S = (2, 3, 6), (4, 5, 7)
        rz = oh[:, 0:8, :].rearrange("p r n -> p (r n)").rearrange("p (q n) -> p q n", q=2)
        n_sb = oh[:, 8:12, :].rearrange("p r n -> p (r n)").rearrange("p (q n) -> p q n", q=2)
        cnt_c = sb("cnt_c", [P, 2, 2])

        names = """consts pads_set edges_in weights_in wt_turned wt_copied wt_stored dve_chain pe_chain
        waited pool_waited totals_ready prefix_done flag_ready win_d_ready win_s_ready diag_ready
        blk_bcast slow_pos pos_s_ready scat_staged rec_d_done win_d_in win_s_in win_turned deg_oh
        deg_mm comb_v comb_t comb_c comb_done seg_oh seg_mm seg_cp seg_ready sg_oh x2_first
        x2_rest gru_rows sg_t sg_cp sg_mm sg_sel sg_ready l0_ready staged one_hot mm accd d_staged
        d_t d_at d_m d_h d_m2 d_h7 d_res x_in wb_in consts_in col_ready col_done gate_step
        gate_done spa_in spa_out pass_ready p_loaded p_split l2_oh l2_t l2_cp l2_p l2_add l2_silu
        l2_c l2_acc sqrt_in sqrt_out x2_done g_agg g_t1 g_a1 g_m g_ag2 g_t2 g_a2 g_ab g_rz g_n
        g_tanh g_xn g_done x3_done final_ready f_res f_out w5_in y_ready""".split()
        S = {n: sem(n) for n in names}
        gd = [sem(f"gathered{i}") for i in range(RING)]
        sc = [sem(f"scattered{i}") for i in range(RING)]
        pair = {n: [sem(f"{n}{q}") for q in range(2)] for n in ("h_out", "x2b_in", "tab_out", "fin_in", "p_in", "y_out")}
        block = ctx.enter_context(nc.Block())

        W_OFF = {"W1": 0, "W2": 512, "ih": 768, "hh": 1536, "F": 2304, "B": 2432}
        NAT = {"W1": (0, 2, 512), "W2": (1024, 2, 256), "ih": (1536, 6, 256), "hh": (3072, 6, 256),
               "F": (4608, 1, 256), "B": (4864, 1, 256)}
        TURN = []
        for name, (a, rows, width) in NAT.items():
            for r in range(rows):
                for c in range(width // P):
                    half = D // P if name == "W1" else 0
                    o = W_OFF[name] + r * P + (c // 2 * D if half else 0)
                    TURN.append((a + r * width + c * P, c % 2, o))

        def dense_rows(dram, block_no):
            return dram[ds(block_no * P, P), :]

        @block.sync
        def _(sp):
            views = {"W1": A["L2_gnn_W1"], "W2": A["L2_gnn_W2"], "ih": A["L2_gnn_w_ih"],
                     "hh": A["L2_gnn_w_hh"], "F": A["L3_gnn_W_f"], "B": A["L3_gnn_W_b"]}
            sp.wait_ge(S["pads_set"], 4)
            CUT = FULL // 16 * 16
            for lo, hi in ((0, CUT), (CUT, FULL)):
                for t, a in ((src_i, "src"), (dst_i, "dst"), (w_nat_e, "edge_weight")):
                    sp.dma_start(t[lo:hi, 0:J], A[a][lo * J:hi * J].rearrange("(p j) -> p j", j=J)).then_inc(S["edges_in"], 16)
                sp.dma_start(dst_next[lo:hi, 0:J], A["dst"][lo * J + 1:hi * J + 1].rearrange("(p j) -> p j", j=J)).then_inc(S["edges_in"], 16)
            for t, a in ((src_i, "src"), (dst_i, "dst"), (w_nat_e, "edge_weight")):
                sp.dma_start(t[FULL:FULL + 1, 0:TAIL], A[a][FULL * J:E].rearrange("(p j) -> p j", p=1)).then_inc(S["edges_in"], 16)
            sp.dma_start(dst_next[FULL:FULL + 1, 0:TAIL - 1], A["dst"][FULL * J + 1:E].rearrange("(p j) -> p j", p=1)).then_inc(S["edges_in"], 16)
            for name, (a, rows, width) in NAT.items():
                sp.dma_start(w_nat[:, a:a + rows * width].rearrange("p (r n) -> p r n", r=rows),
                             views[name].rearrange("(r p) n -> p r n", p=P)).then_inc(S["weights_in"], 16)
            sp.dma_start(wbuf[:, 0:512].rearrange("p (k n) -> p k n", k=2), A["L0_gnn_W6"].rearrange("(k p) n -> p k n", p=P)).then_inc(S["consts_in"], 16)
            bias = {"L0_gnn_b6": 0, "L0_gnn_bp": D}
            for n, o in bias.items():
                sp.dma_start(bias_rows[0:1, o:o + D], A[n].rearrange("(a n) -> a n", a=1)).then_inc(S["consts_in"], 16)
            for k in range(2):
                sp.dma_start(cols[:, k:k + 1], A["L0_gnn_b7"][k * P:(k + 1) * P].rearrange("(p a) -> p a", a=1)).then_inc(S["consts_in"], 16)
            sp.dma_start(cols[:, 2:3], A["L1_gnn_b1"].rearrange("(p a) -> p a", a=1)).then_inc(S["consts_in"], 16)
            sp.dma_start(cols[:, 3:4], A["L1_gnn_gcn_b"].partition_broadcast(P)).then_inc(S["consts_in"], 16)
            sp.dma_start(gw_bc[:, :], A["L1_gnn_gcn_w"].rearrange("n a -> (a n)").partition_broadcast(P)).then_inc(S["consts_in"], 16)
            sp.dma_start(bias_bc[:, :], A["L3_gnn_bias_param"].partition_broadcast(P)).then_inc(S["consts_in"], 16)
            sp.wait_ge(S["wt_copied"], len(TURN))
            for k in range(2):
                sp.dma_start(wt_dram[k], w_tr[:, k, :]).then_inc(S["wt_stored"], 16)
            sp.wait_ge(S["l0_ready"], 1)
            sp.wait_ge(S["scat_staged"], 2 * (J // RING + 1))
            sp.dma_start(x_sb[:, 0:NB - 1, :], A["x"][0:(NB - 1) * P, :].rearrange("(b p) f -> p b f", p=P)).then_inc(S["x_in"], 16)
            sp.dma_start(x_sb[0:LAST, NB - 1, :], A["x"][(NB - 1) * P:N, :]).then_inc(S["x_in"], 16)

            def store_h6(i, q):
                sp.wait_ge(S["d_h"], i * 2 + q + 1 + 2)
                sp.dma_start(dense_rows(h6_dram, i * 2 + q), hq[:, q, :]).then_inc(pair["h_out"][q], 16)
            with sp.Fori(0, PAIRS) as i:
                for q in range(2):
                    store_h6(i, q)
            sp.wait_ge(S["d_m"], NBE + 2)
            sp.dma_start(wbuf[:, 0:512].rearrange("p (k n) -> p k n", k=2), A["L0_gnn_W7"].rearrange("(k p) n -> p k n", p=P)).then_inc(S["wb_in"], 16)
            sp.dma_start(wbuf[:, 512:1024].rearrange("p (k n) -> p k n", k=2), A["L0_gnn_Wp"].rearrange("(k p) n -> p k n", p=P)).then_inc(S["wb_in"], 16)
            sp.wait_ge(S["d_m2"], NBE + 2)
            sp.dma_start(wbuf[:, 0:256].rearrange("p (k n) -> p k n", k=2), A["L1_gnn_w1"].rearrange("(k p) n -> p k n", p=P)).then_inc(S["wb_in"], 16)
            sp.dma_start(wbuf[:, 256:512], A["L1_gnn_w2"]).then_inc(S["wb_in"], 16)
            sp.dma_start(bias_rows[0:1, 0:D], A["L1_gnn_b2"].rearrange("(a n) -> a n", a=1)).then_inc(S["wb_in"], 16)
            sp.dma_start(bias_rows[0:1, D:2 * D], A["L2_gnn_b1"].rearrange("(a n) -> a n", a=1)).then_inc(S["wb_in"], 16)
            sp.wait_ge(S["gate_done"], 1)
            sp.wait_ge(S["wt_stored"], 32)
            sp.dma_start(wbuf[:, 0:1024].rearrange("p (k n) -> p k n", k=2), wt_dram[:, :, 0:512].rearrange("k p n -> p k n")).then_inc(S["wb_in"], 16)
            sp.wait_ge(S["x2_done"], NBE)
            sp.dma_start(x2_dram.rearrange("(b p) f -> p b f", p=P), x_sb).then_inc(S["p_loaded"], 16)
            sp.wait_ge(S["p_loaded"], 16)

            def load_pair(i):
                for q in range(2):
                    sp.wait_ge(S["d_t"], i * 2 + q + 1 + 2 * NBE)
                    sp.dma_start(staged_x[:, q, :], dense_rows(x2_dram, i * 2 + q)).then_inc(pair["p_in"][q], 16)

            def store_q(i):
                for q in range(2):
                    sp.wait_ge(S["d_h"], i * 2 + q + 3 + NBE)
                    sp.dma_start(dense_rows(q_dram, i * 2 + q), hq[:, q, :]).then_inc(pair["tab_out"][q], 16)

            load_pair(0)
            load_pair(1)
            with sp.Fori(2, PAIRS) as i:
                load_pair(i)
                store_q(i - 2)
            store_q(PAIRS - 2)
            store_q(PAIRS - 1)
            sp.wait_ge(S["g_done"], 1)
            sp.dma_start(wih, wt_dram[:, :, 768:1536].rearrange("k p n -> p k n")).then_inc(S["w5_in"], 16)
            sp.dma_start(whh, wt_dram[:, :, 1536:2304].rearrange("k p n -> p k n")).then_inc(S["w5_in"], 16)
            sp.dma_start(w2t, wt_dram[:, :, 512:768].rearrange("k p n -> p k n")).then_inc(S["w5_in"], 16)
            for t, n in ((b2_bc, "L2_gnn_b2"), (gamma_bc, "L2_gnn_gamma"), (beta_bc, "L2_gnn_beta")):
                sp.dma_start(t, A[n].partition_broadcast(P)).then_inc(S["w5_in"], 16)
            sp.dma_start(wbuf[:, 0:512].rearrange("p (k n) -> p k n", k=2), wt_dram[:, :, 2304:2560].rearrange("k p n -> p k n")).then_inc(S["w5_in"], 16)
            for k, n in enumerate(("L2_gnn_b_ih", "L2_gnn_b_hh")):
                sp.dma_start(gru_bias[:, 3 * D * k:3 * D * (k + 1)], A[n].partition_broadcast(3)).then_inc(S["w5_in"], 16)
            x2_rows = x2_dram.rearrange("(b p) f -> p b f", p=P)
            sp.dma_start(x_sb[:, 0:2, :], x2_rows[:, 0:2, :]).then_inc(S["x2_first"], 16)
            sp.dma_start(x_sb[:, 2:NBE, :], x2_rows[:, 2:NBE, :]).then_inc(S["x2_rest"], 16)
            sp.wait_ge(S["g_xn"], NBE + 2)
            with sp.Fori(0, PAIRS) as i:
                for q in range(2):
                    sp.wait_ge(S["f_res"], i * 2 + q + 1)
                    sp.dma_start(hq[:, q, :], dense_rows(x2_dram, i * 2 + q)).then_inc(pair["x2b_in"][q], 16)
            sp.wait_ge(S["f_res"], NBE + 2)
            with sp.Fori(0, PAIRS) as i:
                for q in range(2):
                    n = i * 2 + q
                    sp.wait_ge(S["d_h"], n + 3 + 2 * NBE)
                    sp.dma_start(dense_rows(fwd_dram, n), hq[:, q, 0:P]).then_inc(pair["tab_out"][q], 16)
                    sp.dma_start(dense_rows(bwd_dram, n), hq[:, q, P:D]).then_inc(pair["tab_out"][q], 16)
            sp.wait_ge(S["final_ready"], 1)
            with sp.Fori(0, PAIRS) as i:
                for q in range(2):
                    n = i * 2 + q
                    sp.wait_ge(S["f_out"], n + 1)
                    sp.dma_start(hq[:, q, 0:P], dense_rows(fwd_dram, n)).then_inc(pair["fin_in"][q], 16)
                    sp.dma_start(hq[:, q, P:D], dense_rows(bwd_dram, n)).then_inc(pair["fin_in"][q], 16)
            with sp.Fori(0, PAIRS - 1) as i:
                for q in range(2):
                    sp.wait_ge(S["y_ready"], i * 2 + q + 1)
                    sp.dma_start(dense_rows(out, i * 2 + q), staged_x[:, q, :]).then_inc(pair["y_out"][q], 16)
            sp.wait_ge(S["y_ready"], 2 * (PAIRS - 1) + 1)
            sp.dma_start(out[(NB - 1) * P:N, :], staged_x[0:LAST, 0, :]).then_inc(pair["y_out"][0], 16)
            sp.wait_ge(pair["y_out"][0], 16 * PAIRS)
            sp.wait_ge(pair["y_out"][1], 16 * (PAIRS - 1))

        @block.gpsimd
        def _(pool):
            pool.memset(ident[:, :], 0.0).then_inc(S["consts"], 1)
            pool.memset(ones[:, :], 1.0).then_inc(S["consts"], 1)
            pool.memset(before[:, :], 1.0).then_inc(S["consts"], 1)
            pool.wait_ge(S["consts"], 3)
            pool.affine_select(out=ident[:, :], in_=ident[:, :], compare_op=ALU.not_equal, fill=1.0, base=0,
                               pattern=[[-1, P]], channel_multiplier=1).then_inc(S["consts"], 1)
            pool.affine_select(out=before[:, :], in_=before[:, :], compare_op=ALU.is_gt, fill=0.0, base=0,
                               pattern=[[1, P]], channel_multiplier=-1).then_inc(S["consts"], 1)
            pool.iota(iota_i[:, :], pattern=[[1, P]], base=0, channel_multiplier=0).then_inc(S["consts"], 1)
            pool.iota(tile_no_i[:, :], pattern=[[P, TG]], base=0, channel_multiplier=1).then_inc(S["consts"], 1)
            pool.iota(node_i[:, :], pattern=[[P, NBE]], base=0, channel_multiplier=1).then_inc(S["consts"], 1)
            pool.iota(pos_start[:, :], pattern=[[1, J]], base=0, channel_multiplier=J).then_inc(S["consts"], 1)

            def windows(rec, index, win, done):
                rows = rec.rearrange("(r s) w -> r (s w)", s=CHUNK)
                flat = win.rearrange("p g s w -> p g (s w)")
                for g in range(TG):
                    for k in range(P // CHUNK):
                        w = CHUNK * WORDS
                        pool.indirect_dma_start(out=flat[:, g, k * w:(k + 1) * w], out_offset=None, in_=rows,
                                                in_offset=bass.IndirectOffsetOnAxis(ap=index[:, g, k:k + 1], axis=0)).then_inc(done, 16)

            pool.wait_ge(S["flag_ready"], 1)
            unsorted = pool.value_load(flag_i[0:1, 0:1], min_val=0, max_val=E)
            with pool.If(unsorted > 0):
                pool.wait_ge(S["slow_pos"], 1)

                def scatter_slowly(j, first):
                    if not first:
                        pool.wait_ge(S["rec_d_done"], j * 16)
                    pool.tensor_copy(stage_i[:, 0, 0:1], pos_d[:, ds(j, 1)]).then_inc(S["slow_pos"], 1)
                    pool.tensor_copy(stage_r[:, 0, 0, :], pay[:, ds(j, 1), :].rearrange("p a w -> p (a w)")).then_inc(S["slow_pos"], 1)
                    pool.wait_ge(S["slow_pos"], j * 2 + 3)
                    apart(pool, S["pool_waited"])
                    pool.indirect_dma_start(out=rec_d, out_offset=bass.IndirectOffsetOnAxis(ap=stage_i[:, 0, 0:1], axis=0),
                                            in_=stage_r[:, 0, 0, :], in_offset=None).then_inc(S["rec_d_done"], 16)

                scatter_slowly(0, True)
                with pool.Fori(1, J) as j:
                    scatter_slowly(j, False)
                pool.wait_ge(S["rec_d_done"], J * 16)
            with pool.Else():
                pool.dma_start(rec_d.rearrange("(p j) w -> p (j w)", j=J), pay[:, 0:J, :].rearrange("p j w -> p (j w)")).then_inc(S["rec_d_done"], 16)
                pool.wait_ge(S["rec_d_done"], 16)
            pool.wait_ge(S["win_d_ready"], 1)
            windows(rec_d, win_i_d, win_d, S["win_d_in"])

            def stage_scatter(first, v):
                pool.tensor_copy(stage_i[:, v, :], pos_s[:, ds(first, RING)]).then_inc(S["scat_staged"], 1)
                pool.tensor_copy(stage_r[:, v, :, :], pay[:, ds(first, RING), :]).then_inc(S["scat_staged"], 1)

            def scatter_turn(i, first):
                for v in range(3):
                    pool.wait_ge(S["scat_staged"], i * 6 + 2 * v + 2)
                    apart(pool, S["pool_waited"])
                    for u in range(RING):
                        if not (first and v == 0):
                            pool.wait_ge(sc[u], i * 48 + 16 * v)
                            apart(pool, S["pool_waited"])
                        pool.indirect_dma_start(out=rec_s, out_offset=bass.IndirectOffsetOnAxis(ap=stage_i[:, v, u:u + 1], axis=0),
                                                in_=stage_r[:, v, u, :], in_offset=None).then_inc(sc[u], 16)
                        if u == RING // 2 - 1:
                            stage_scatter(i * SPAN + RING * (v + 1), (v + 1) % 3)

            turns = J // SPAN
            pool.wait_ge(S["pos_s_ready"], 1)
            stage_scatter(0, 0)
            scatter_turn(0, True)
            with pool.Fori(1, turns) as i:
                scatter_turn(i, False)
            for u in range(RING):
                pool.wait_ge(sc[u], 48 * turns)
            pool.wait_ge(S["win_s_ready"], 1)
            pool.wait_ge(S["wt_stored"], 32)
            windows(rec_s, win_i_s, win_s, S["win_s_in"])

            def gathers(k, table, width, index, free, base, together=1):
                def stage(first, v):
                    pool.tensor_copy(stage_i[:, v, :], index[:, ds(first, RING)]).then_inc(S["staged"], 1)

                rounds = (T // RING + 1) * k
                if k:
                    pool.wait_ge(S["staged"], rounds)
                stage(0, 0)
                with pool.Fori(0, TURNS) as i:
                    for u in range(SPAN):
                        v = u // RING
                        if u % RING == 0:
                            pool.wait_ge(S["staged"], i * 3 + rounds + v + 1)
                        pool.wait_ge(free, i * (SPAN // together) + base + u // together + 1)
                        apart(pool, S["pool_waited"])
                        pool.indirect_dma_start(out=gbuf[:, u % RING, 0:width], out_offset=None, in_=table,
                                                in_offset=bass.IndirectOffsetOnAxis(ap=stage_i[:, v, u % RING:u % RING + 1], axis=0)).then_inc(gd[u % RING], 16)
                        if u % RING == RING // 2 - 1:
                            stage(i * SPAN + RING * (v + 1), (v + 1) % 3)

            pool.wait_ge(S["l0_ready"], 1)
            pool.wait_ge(S["scat_staged"], 2 * (J // RING + 1))
            gathers(0, A["x"], D, d_idx, S["mm"], 0)
            for q in range(2):
                pool.wait_ge(pair["h_out"][q], 16 * PAIRS)
            gathers(1, h6_dram, D, d_idx, S["mm"], T)
            for q in range(2):
                pool.wait_ge(pair["tab_out"][q], 16 * PAIRS)
            gathers(2, q_dram, D, s_idx, S["l2_add"], 0, 2)
            for q in range(2):
                pool.wait_ge(pair["tab_out"][q], 48 * PAIRS)
            gathers(3, fwd_dram, P, s_idx, S["mm"], 2 * T)
            gathers(4, bwd_dram, P, d_idx, S["mm"], 3 * T)

        @block.tensor
        def _(pe):
            regs = [pe.alloc_register(f"pe_blk{j}") for j in range(8)]
            pe.sem_inc(S["mm"], 8)
            pe.sem_inc(S["seg_mm"], 3)
            pe.sem_inc(S["deg_mm"], 2)
            pe.sem_inc(S["sg_t"], 3)
            pe.sem_inc(S["sg_mm"], 3)
            pe.sem_inc(S["d_t"], 2)
            pe.sem_inc(S["d_m"], 2)
            pe.sem_inc(S["d_m2"], 2)
            pe.sem_inc(S["l2_p"], 4)
            pe.sem_inc(S["l2_c"], 12)
            for n in ("g_t1", "g_m", "g_t2", "g_ab"):
                pe.sem_inc(S[n], 2)

            pe.wait_ge(S["consts"], 9)
            pe.wait_ge(S["weights_in"], 16 * len(NAT))
            for m, (a, _, _) in enumerate(TURN):
                if m >= 4:
                    pe.wait_ge(S["wt_copied"], m - 3)
                pe.transpose(bank[4 + m % 4][:, 0:P], w_nat[:, a:a + P], ident[:, :]).then_inc(S["wt_turned"], 1)
            pe.wait_ge(S["totals_ready"], 1)
            for k, tot in enumerate((sm["tot_d"], sm["tot_s"])):
                pe.matmul(bank[k][:, 0:NB], before[:, :], tot[:, 0:NB], start=True, stop=True)
                pe.matmul(bank[k][:, 64:64 + NB], ones[:, :], tot[:, 0:NB], start=True, stop=True)
            pe.matmul(bank[1][:, 128:129], ones[:, :], viol[:, :], start=True, stop=True).then_inc(S["prefix_done"], 1)
            for k in range(2):
                for g in range(TG):
                    pe.wait_ge(S["diag_ready"], k * TG + g + 1)
                    pe.matmul(bank[2 + g // 4][:, g % 4 * P:(g % 4 + 1) * P], ones[:, :], diag[:, g % 2, :],
                              start=True, stop=True).then_inc(S["blk_bcast"], 1)

            def turn_windows(win, words, done, fills):
                pe.wait_ge(done, 16 * TG * (P // CHUNK))
                for w in range(words):
                    for lo in range(0, TG, 4):
                        b = 4 + fills % 4
                        pe.wait_ge(S["wt_copied"], len(TURN) + fills - 3)
                        for g in range(lo, min(lo + 4, TG)):
                            mm = pe.transpose(bank[b][:, (g - lo) * P:(g - lo + 1) * P], win[:, g, :, w], ident[:, :])
                        mm.then_inc(S["win_turned"], 1)
                        fills += 1
                return fills

            fills = turn_windows(win_d, 3, S["win_d_in"], 0)

            def segment_sums(k):
                pe.wait_ge(S["seg_ready"], k + 1)
                with pe.Fori(0, TURNS) as i:
                    for g in range(GROUPS):
                        m = i * GROUPS + T // GROUP * k + g
                        pe.wait_ge(S["seg_cp"], m + 1)
                        pe.wait_ge(S["seg_oh"], m + 1)
                        for u in range(GROUP):
                            mm = pe.matmul(bank[2 + g % 2][:, u * 4:u * 4 + 4], ohb[:, g % 3 * GROUP + u, :],
                                           parts[:, ds(i * SPAN + 4 * g + u, 1), :].rearrange("p a w -> p (a w)"), start=True, stop=True)
                        mm.then_inc(S["seg_mm"], 1)

            def combine(k, turns):
                for g in range(TG):
                    pe.wait_ge(S["comb_v"], k + 1)
                    mm = pe.transpose(bank[4 + g // 4][:, g % 4 * P:(g % 4 + 1) * P], val_b[:, g * P:(g + 1) * P], ident[:, :])
                    if g in (3, TG - 1):
                        mm.then_inc(S["comb_t"], 1)
                pe.wait_ge(S["comb_c"], 2 * k + 2)
                for g in range(TG):
                    mm = pe.matmul(bank[1][:, 0:NB], val_a[:, g * P:(g + 1) * P], tile_oh[:, g, :], start=(g == 0), stop=(g == TG - 1))
                mm.then_inc(S["comb_done"], 1)

            segment_sums(0)
            combine(0, 0)
            combine(1, 0)
            pe.matmul(bank[0][:, 0:NB], ones[:, :], zeros[:, 0:NB], start=True, stop=False, skip_group_check=True)
            with pe.Fori(0, J // SPAN) as i:
                for g in range(GROUPS):
                    pe.wait_ge(S["deg_oh"], i * GROUPS + g + 1)
                    for u in range(GROUP):
                        v = g % 2 * GROUP + u
                        mm = pe.matmul(bank[0][:, 0:NB], oh[:, 4 + v, :], junk[:, v, 0:NB], start=False, stop=False, skip_group_check=True)
                    mm.then_inc(S["deg_mm"], 1)

            def node_values(k):
                pe.wait_ge(S["sg_ready"], k + 1)

                def turn_of(i, first, last):
                    for g in range(2 if last else GROUPS):
                        m = i * GROUPS + T // GROUP * k + g
                        if not last:
                            pe.wait_ge(S["sg_oh"], m + 1)
                            pe.wait_ge(S["sg_cp"], m + 1)
                            b = bank[SG_T[g % 3]][:, 0:256].bitcast(BF16)
                            for u in range(GROUP):
                                mm = pe.transpose(b[:, u * P:(u + 1) * P], ohb[:, g % 3 * GROUP + u, :], ident_b[:, :])
                            mm.then_inc(S["sg_t"], 1)
                        if runs(g, 2, first, last):
                            h = (g - 2) % 3
                            pe.wait_ge(S["sg_cp"], m - 2 + 1 + 3)
                            pe.wait_ge(S["sg_sel"], m - 2 + 1)
                            for u in range(GROUP):
                                for s in range(3):
                                    mm = pe.matmul(bank[SG_S[h]][:, u * 64:u * 64 + NB], oht[:, h, u * P:(u + 1) * P], table3[:, s, 0:NB],
                                                   start=(s == 0), stop=(s == 2))
                            mm.then_inc(S["sg_mm"], 1)

                in_turns(pe, TURNS, turn_of, 2)
                pe.wait_ge(S["sg_sel"], T // GROUP * (k + 1) + 3)

            node_values(0)
            node_values(1)
            fills = turn_windows(win_s, 2, S["win_s_in"], fills)

            def scatter_pass(k, kk, width):
                with pe.Fori(0, TURNS) as i:
                    for u in range(SPAN):
                        n = i * SPAN + T * kk + u
                        pe.wait_ge(S["one_hot"], n + 1)
                        pe.wait_ge(gd[u % RING], i * 48 + 16 * (T // RING * k + u // RING + 1))
                        pe.wait_ge(S["accd"], n + 1)
                        pe.matmul(bank[u % 4][:, 0:width], oh[:, u % 4, :], gbuf[:, u % RING, 0:width],
                                  start=True, stop=True).then_inc(S["mm"], 1)

            def turn(n, q, src, b):
                for k in range(2):
                    mm = pe.transpose(bank[b][:, k * P:(k + 1) * P], src[:, k * P:(k + 1) * P], ident[:, :])
                mm.then_inc(S["d_t"], 1)

            w0, w1 = (wbuf[:, 512 * k:512 * (k + 1)].rearrange("p (k n) -> p k n", k=2) for k in range(2))
            scatter_pass(0, 0, D)
            pe.wait_ge(S["consts_in"], 16 * 9)
            def d1_products(i, first, last):
                if not last:
                    for q in range(2):
                        n = i * 2 + q
                        pe.wait_ge(S["d_staged"], n + 1)
                        pe.wait_ge(S["d_at"], n + 1)
                        turn(n, q, staged_x[:, q, :], 4 + q)
                if first:
                    return
                for q in range(2):
                    n = i * 2 - 2 + q
                    pe.wait_ge(S["d_at"], n + 1 + 2)
                    pe.wait_ge(S["d_h"], n + 1)
                    for k in range(2):
                        pe.matmul(bank[6 + q][:, 0:D], turned[:, q, k * P:(k + 1) * P], w0[:, k, :], start=(k == 0), stop=False)
                    pe.matmul(bank[6 + q][:, 0:D], ones[0:1, :], bias_rows[0:1, 0:D], start=False, stop=True).then_inc(S["d_m"], 1)

            in_turns(pe, PAIRS, d1_products, 1)
            scatter_pass(1, 1, D)
            pe.wait_ge(S["wb_in"], 32)
            with pe.Fori(0, PAIRS) as i:
                for q in range(2):
                    n = i * 2 + q + NBE
                    pe.wait_ge(S["d_staged"], n + 1)
                    pe.wait_ge(S["d_at"], n + 1)
                    turn(n, q, staged_x[:, q, :], 4 + q)
                for q in range(2):
                    n = i * 2 + q + NBE
                    pe.wait_ge(S["d_at"], n + 1 + 2)
                    pe.wait_ge(S["d_h7"], i * 2 + q + 1)
                    for o in range(2):
                        for k in range(2):
                            mm = pe.matmul(bank[6 + q][:, o * P:(o + 1) * P], w0[:, k, o * P:(o + 1) * P], turned[:, q, k * P:(k + 1) * P],
                                           start=(k == 0), stop=(k == 1))
                    mm.then_inc(S["d_m"], 1)
                for q in range(2):
                    n = i * 2 + q
                    pe.wait_ge(S["d_h7"], n + 1 + 2)
                    pe.wait_ge(S["d_res"], n + 1)
                    for k in range(2):
                        pe.matmul(bank[2 + q][:, 0:D], h7t[:, q, k * P:(k + 1) * P], w1[:, k, :], start=(k == 0), stop=False)
                    pe.matmul(bank[2 + q][:, 0:D], ones[0:1, :], bias_rows[0:1, D:2 * D], start=False, stop=True).then_inc(S["d_m2"], 1)
            pe.matmul(bank[0][0:1, 256:256 + D], ones[:, 0:1], zeros[:, :], start=True, stop=False, skip_group_check=True)
            with pe.Fori(0, NBE) as b:
                pe.wait_ge(S["col_ready"], b + 1)
                pe.matmul(bank[0][0:1, 256:256 + D], ones[:, 0:1], x_sb[:, ds(b, 1), :].rearrange("p a f -> p (a f)"),
                          start=False, stop=False, skip_group_check=True).then_inc(S["col_done"], 1)
            pe.wait_ge(S["wb_in"], 32 + 64)
            pe.wait_ge(S["gate_step"], 1)
            for k in range(2):
                mm = pe.matmul(bank[1][:, k:k + 1], staged_x[0:1, 0, k * P:(k + 1) * P], ones[0:1, 0:1], start=True, stop=True)
            mm.then_inc(S["pe_chain"], 1)
            pe.wait_ge(S["gate_step"], 2)
            for k in range(2):
                mm = pe.matmul(bank[1][:, 4:5], wbuf[:, k * P:(k + 1) * P], cols[:, 4 + k:5 + k], start=(k == 0), stop=(k == 1))
            mm.then_inc(S["pe_chain"], 1)
            pe.wait_ge(S["gate_step"], 3)
            pe.matmul(bank[1][0:1, 128:128 + D], cols[:, 6:7], wbuf[:, 256:512], start=True, stop=False)
            pe.matmul(bank[1][0:1, 128:128 + D], ones[0:1, 0:1], bias_rows[0:1, 0:D], start=False, stop=True).then_inc(S["pe_chain"], 1)
            pe.wait_ge(S["gate_step"], 4)
            pe.matmul(bank[4][:, 0:D], ones[0:1, :], staged_x[0:1, 1, :], start=True, stop=True).then_inc(S["pe_chain"], 1)

            node_values(2)
            segment_sums(1)
            combine(2, 0)

            pe.wait_ge(S["wb_in"], 32 + 64 + 16)
            w_ab = wbuf[:, 0:1024].rearrange("p (k n) -> p k n", k=2)

            def d4_products(i, first, last):
                if not last:
                    for q in range(2):
                        n = i * 2 + q + 2 * NBE
                        pe.wait_ge(pair["p_in"][q], i * 16 + 16)
                        pe.wait_ge(S["d_at"], n + 1)
                        turn(n, q, staged_x[:, q, :], 4 + q)
                if first:
                    return
                for q in range(2):
                    n = i * 2 - 2 + q
                    pe.wait_ge(S["d_at"], n + 1 + 2 + 2 * NBE)
                    pe.wait_ge(S["d_h"], n + 1 + NBE)
                    pe.wait_ge(S["p_split"], n + 1)
                    for k in range(2):
                        pe.matmul(bank[2 + q][:, 0:D], turned[:, q, k * P:(k + 1) * P], w_ab[:, k, D:2 * D], start=(k == 0), stop=(k == 1))
                    for k in range(2):
                        pe.matmul(bank[6 + q][:, 0:D], turned[:, q, k * P:(k + 1) * P], w_ab[:, k, 0:D], start=(k == 0), stop=False)
                    pe.matmul(bank[6 + q][:, 0:D], ones[0:1, :], bias_rows[0:1, D:2 * D], start=False, stop=True).then_inc(S["d_m"], 1)

            in_turns(pe, PAIRS, d4_products, 1)

            pe.wait_ge(S["pass_ready"], 1)

            def l2_products(i, first, last):
                for g in range(2 if last else GROUPS):
                    m = i * GROUPS + g
                    if runs(g, 1, first, last):
                        h = g - 1
                        if h % 2 == 0:
                            pe.load(regs, blk_s[0:1, ds(i * SPAN + 4 * h, 8)])
                        pe.wait_ge(S["l2_cp"], m - 1 + 1 + 2)
                        for u in range(GROUP):
                            b = pe.snap(regs[4 * (h % 2) + u], min_val=0, max_val=NB - 1)
                            if u % 2 == 0:
                                pe.wait_ge(S["l2_add"], i * (SPAN // 2) + 2 * h + u // 2 + 3)
                            for s in range(3):
                                mm = pe.matmul(bank[2 + u // 2][:, u % 2 * D:(u % 2 + 1) * D], oht[:, h % 2, u * P:(u + 1) * P],
                                               p3[:, s, ds(b, 1), :].rearrange("p a f -> p (a f)"), start=(s == 0), stop=(s == 2))
                            if u % 2:
                                mm.then_inc(S["l2_p"], 1)
                    if not last:
                        pe.wait_ge(S["l2_oh"], i * SPAN + 4 * g + 4)
                        pe.wait_ge(S["l2_cp"], m + 1)
                        for u in range(GROUP):
                            mm = pe.transpose(bank[g % 2][:, u * P:(u + 1) * P], oh[:, (4 * g + u) % 12, :], ident[:, :])
                        mm.then_inc(S["l2_t"], 1)
                    if runs(g, 2, first, last):
                        for u in range(GROUP):
                            t = 4 * (g - 2) + u
                            pe.wait_ge(S["l2_silu"], i * (SPAN // 2) + t // 2 + 1)
                            pe.wait_ge(S["l2_acc"], i * SPAN + t + 1)
                            pe.matmul(bank[4 + u][:, 0:D + 1], oh[:, t % 12, :], msg[:, t % RING, :], start=True, stop=True).then_inc(S["l2_c"], 1)

            in_turns(pe, TURNS, l2_products, 2)

            pe.wait_ge(S["w5_in"], 16 * 9)
            pe.wait_ge(S["gru_rows"], 1)

            def candidate_and_gates(n, q):
                A_b, B_b = bank[3 + 2 * q], bank[4 + 2 * q]
                pe.wait_ge(S["g_a2"], n + 1 + 2)
                pe.wait_ge(S["g_tanh"], n + 1)
                for k in range(2):
                    pe.matmul(A_b[:, :], turned[:, q, k * P:(k + 1) * P], wih[:, k, 0:2 * D], start=(k == 0), stop=False)
                    pe.matmul(A_b[:, :], turned[:, q, (2 + k) * P:(3 + k) * P], whh[:, k, 0:2 * D], start=False, stop=False)
                pe.matmul(A_b[:, :], ones_b[:, :], gru_rows[:, 0:2 * D], start=False, stop=False)
                pe.matmul(A_b[:, :], ones_b[:, :], gru_rows[:, 3 * D:5 * D], start=False, stop=True)
                for k in range(2):
                    pe.matmul(B_b[:, 0:D], turned[:, q, k * P:(k + 1) * P], wih[:, k, 2 * D:3 * D], start=(k == 0), stop=False)
                pe.matmul(B_b[:, 0:D], ones_b[:, :], gru_rows[:, 2 * D:3 * D], start=False, stop=True)
                for k in range(2):
                    pe.matmul(B_b[:, D:2 * D], turned[:, q, (2 + k) * P:(3 + k) * P], whh[:, k, 2 * D:3 * D], start=(k == 0), stop=False)
                pe.matmul(B_b[:, D:2 * D], ones_b[:, :], gru_rows[:, 5 * D:6 * D], start=False, stop=True).then_inc(S["g_ab"], 1)

            def gru_products(i, first, last):
                if not last:
                    for q in range(2):
                        n = i * 2 + q
                        pe.wait_ge(S["g_agg"], n + 1)
                        pe.wait_ge(S["g_a1"], n + 1)
                        pe.wait_ge(S["g_ag2"], n + 1)
                        for k in range(2):
                            mm = pe.transpose(bank[q][:, k * P:(k + 1) * P], staged_x[:, q, k * P:(k + 1) * P], ident[:, :])
                        mm.then_inc(S["g_t1"], 1)
                if not first:
                    candidate_and_gates(i * 2 - 2, 0)
                if not last:
                    for q in range(2):
                        pe.wait_ge(S["g_a1"], i * 2 + q + 1 + 2)
                        for k in range(2):
                            mm = pe.matmul(bank[q][:, D:2 * D], h7t[:, q, k * P:(k + 1) * P], w2t[:, k, :], start=(k == 0), stop=(k == 1))
                        mm.then_inc(S["g_m"], 1)
                if not first:
                    candidate_and_gates(i * 2 - 1, 1)
                if not last:
                    for q in range(2):
                        n = i * 2 + q
                        b = bank[2] if q == 0 else bank[7]
                        pe.wait_ge(S["g_ag2"], n + 1 + 2)
                        pe.wait_ge(S["g_a2"], n + 1)
                        for k in range(2):
                            pe.transpose(b[:, k * P:(k + 1) * P], tmp_q[:, q, k * P:(k + 1) * P], ident[:, :])
                        for k in range(2):
                            mm = pe.transpose(b[:, (2 + k) * P:(3 + k) * P], hq[:, q, k * P:(k + 1) * P], ident[:, :])
                        mm.then_inc(S["g_t2"], 1)

            in_turns(pe, PAIRS, gru_products, 1)

            def d6_products(i, first, last):
                if not last:
                    for q in range(2):
                        n = i * 2 + q + 2 * NBE
                        pe.wait_ge(S["d_staged"], n + 1)
                        pe.wait_ge(S["d_at"], n + 1 + NBE)
                        turn(n, q, staged_x[:, q, :], 4 + q)
                if first:
                    return
                for q in range(2):
                    n = i * 2 - 2 + q
                    pe.wait_ge(S["d_at"], n + 1 + 2 + 3 * NBE)
                    pe.wait_ge(S["d_h"], n + 1 + 2 * NBE)
                    for k in range(2):
                        mm = pe.matmul(bank[6 + q][:, 0:D], turned[:, q, k * P:(k + 1) * P], w0[:, k, :], start=(k == 0), stop=(k == 1))
                    mm.then_inc(S["d_m"], 1)

            in_turns(pe, PAIRS, d6_products, 1)
            scatter_pass(3, 2, P)
            scatter_pass(4, 3, P)

        @block.scalar
        def _(act):
            act.sem_inc(S["sg_cp"], 3)
            for n in ("seg_cp", "d_at", "d_h", "d_h7", "l2_cp", "g_a1", "g_a2", "g_tanh"):
                act.sem_inc(S[n], 2)
            for m, (_, k, o) in enumerate(TURN):
                act.wait_ge(S["wt_turned"], m + 1)
                act.activation(w_tr[:, k, o:o + P], bank[4 + m % 4][:, 0:P], ACT.Copy).then_inc(S["wt_copied"], 1)

            def copy_windows(dests, fills):
                for dst in dests:
                    for lo in range(0, TG, 4):
                        n = min(4, TG - lo) * P
                        act.wait_ge(S["win_turned"], fills + 1)
                        act.activation(dst[:, lo * P:lo * P + n], bank[4 + fills % 4][:, 0:n], ACT.Copy).then_inc(S["wt_copied"], 1)
                        fills += 1
                return fills

            def copy_sums(k):
                with act.Fori(0, TURNS) as i:
                    for g in range(GROUPS):
                        act.wait_ge(S["seg_mm"], i * GROUPS + T // GROUP * k + g + 1 + 3)
                        act.activation(tile_sums[:, ds(i * SPAN + 4 * g, 4), :].rearrange("p t w -> p (t w)"),
                                       bank[2 + g % 2][:, 0:16], ACT.Copy).then_inc(S["seg_cp"], 1)

            def copy_combine(k):
                for h in range(2):
                    n = (4 if h == 0 else TG - 4) * P
                    act.wait_ge(S["comb_t"], 2 * k + h + 1)
                    act.activation(val_a[:, h * 4 * P:h * 4 * P + n], bank[4 + h][:, 0:n], ACT.Copy).then_inc(S["comb_c"], 1)

            def copy_turned(k):
                with act.Fori(0, TURNS) as i:
                    for g in range(GROUPS):
                        m = i * GROUPS + T // GROUP * k + g
                        act.wait_ge(S["sg_t"], m + 1 + 3)
                        act.wait_ge(S["sg_mm"], m + 1)
                        act.activation(oht[:, g % 3, :], bank[SG_T[g % 3]][:, 0:256].bitcast(BF16), ACT.Copy).then_inc(S["sg_cp"], 1)

            sqrts = [0]

            def square_root(x):
                sqrts[0] += 1
                act.wait_ge(S["sqrt_in"], sqrts[0])
                act.activation(x, x, ACT.Sqrt).then_inc(S["sqrt_out"], 1)

            fills = copy_windows((d_idx, d_loc, d_norm), 0)
            copy_sums(0)
            copy_combine(0)
            copy_combine(1)
            copy_turned(0)
            copy_turned(1)
            square_root(val_a[:, 0:T])
            fills = copy_windows((s_loc, s_idx), fills)

            def copy_block(n, q):
                act.wait_ge(S["d_t"], n + 1 + 2)
                act.wait_ge(S["d_m"], n + 1)
                act.activation(turned[:, q, 0:D], bank[4 + q][:, 0:D], ACT.Copy).then_inc(S["d_at"], 1)

            def outputs_of(i, first, last, base, stored, from_bank, function):
                for q in range(2):
                    if not last:
                        copy_block(i * 2 + q + base, q)
                    if not first:
                        act.wait_ge(S["d_m"], i * 2 - 2 + q + base + 1 + 2)
                        if stored != "none":
                            act.wait_ge(pair[stored][q], i * 16 - 16)
                        act.activation(hq[:, q, :], bank[from_bank + q][:, 0:D], function).then_inc(S["d_h"], 1)

            def pairs_of_outputs(base, stored, from_bank, function):
                outputs_of(0, True, False, base, stored, from_bank, function)
                outputs_of(1, False, False, base, "none", from_bank, function)
                with act.Fori(2, PAIRS) as i:
                    outputs_of(i, False, False, base, stored, from_bank, function)
                outputs_of(PAIRS, False, True, base, stored, from_bank, function)

            pairs_of_outputs(0, "h_out", 6, ACT.Relu)
            with act.Fori(0, PAIRS) as i:
                for q in range(2):
                    copy_block(i * 2 + q + NBE, q)
                for q in range(2):
                    n = i * 2 + q
                    act.wait_ge(S["d_m"], n + NBE + 1 + 2)
                    act.wait_ge(S["d_m2"], n + 1)
                    act.activation(h7t[:, q, 0:P], bank[6 + q][:, 0:P], ACT.Relu, bias=cols[:, 0:1])
                    act.activation(h7t[:, q, P:D], bank[6 + q][:, P:D], ACT.Relu, bias=cols[:, 1:2]).then_inc(S["d_h7"], 1)
            square_root(sm["rstd"][:, 0:NBE])
            square_root(sm["t_a"][:, 0:NBE])
            act.wait_ge(S["gate_step"], 1)
            act.wait_ge(S["pe_chain"], 1)
            act.activation(cols[:, 4:6], bank[1][:, 0:2], ACT.Copy).then_inc(S["gate_step"], 1)
            act.wait_ge(S["pe_chain"], 2)
            act.activation(cols[:, 6:7], bank[1][:, 4:5], ACT.Relu, bias=cols[:, 2:3]).then_inc(S["gate_step"], 1)
            act.wait_ge(S["pe_chain"], 3)
            act.activation(staged_x[0:1, 1, :], bank[1][0:1, 128:128 + D], ACT.Sigmoid).then_inc(S["gate_step"], 1)
            copy_turned(2)
            copy_sums(1)
            copy_combine(2)
            act.wait_ge(S["spa_in"], 1)
            act.activation(sm["spa"][:, 0:NB], sm["spa"][:, 0:NB], ACT.Sigmoid, bias=cols[:, 3:4]).then_inc(S["spa_out"], 1)
            square_root(sm["rstd"][:, 0:NBE])

            pairs_of_outputs(2 * NBE, "tab_out", 2, ACT.Copy)

            def l2_functions(i, first, last):
                for g in range(1 if last else GROUPS):
                    if not last:
                        act.wait_ge(S["l2_t"], i * GROUPS + g + 1)
                        act.wait_ge(S["l2_p"], i * (SPAN // 2) + 2 * g + 2)
                        act.activation(oht[:, g % 2, :], bank[g % 2][:, :], ACT.Copy).then_inc(S["l2_cp"], 1)
                    if runs(g, 1, first, last):
                        for t in range(4 * (g - 1), 4 * g, 2):
                            act.wait_ge(S["l2_add"], i * (SPAN // 2) + t // 2 + 1 + 4)
                            both = msg[:, t % RING:t % RING + 2, 0:D]
                            act.activation(both, both, ACT.Silu).then_inc(S["l2_silu"], 1)

            in_turns(act, TURNS, l2_functions, 1)

            def copy_state(n, q):
                act.wait_ge(S["g_t2"], n + 1 + 2)
                act.wait_ge(S["g_ab"], n + 1)
                act.activation(turned[:, q, :], (bank[2] if q == 0 else bank[7])[:, :], ACT.Copy).then_inc(S["g_a2"], 1)

            def gates(n, q):
                act.wait_ge(S["g_ab"], n + 1 + 2)
                act.wait_ge(S["g_xn"], n + 1)
                act.activation(rz[:, q, :], bank[3 + 2 * q][:, :], ACT.Sigmoid).then_inc(S["g_rz"], 1)

            def candidate(n, q):
                act.wait_ge(S["g_n"], n + 1)
                act.activation(n_sb[:, q, :], n_sb[:, q, :], ACT.Tanh).then_inc(S["g_tanh"], 1)

            def gru_functions(i, first, last):
                if not last:
                    for q in range(2):
                        n = i * 2 + q
                        act.wait_ge(S["g_t1"], n + 1 + 2)
                        act.wait_ge(S["g_m"], n + 1)
                        act.activation(h7t[:, q, :], bank[q][:, 0:D], ACT.Copy).then_inc(S["g_a1"], 1)
                if not first:
                    gates(i * 2 - 2, 0)
                    candidate(i * 2 - 2, 0)
                    gates(i * 2 - 1, 1)
                if not last:
                    copy_state(i * 2, 0)
                if not first:
                    candidate(i * 2 - 1, 1)
                if not last:
                    copy_state(i * 2 + 1, 1)

            in_turns(act, PAIRS, gru_functions, 1)
            square_root(sm["rstd"][:, 0:NBE])
            square_root(sm["rstd"][:, 0:NBE])
            square_root(sm["t_a"][:, 0:NBE])
            with act.Fori(0, PAIRS) as i:
                for q in range(2):
                    copy_block(i * 2 + q + 3 * NBE, q)
            square_root(sm["rstd"][:, 0:NBE])

        @block.vector
        def _(dve):
            chain = Chain(dve, S["dve_chain"])
            link = chain.link
            regs = [dve.alloc_register(f"dve_blk{j}") for j in range(8)]
            dve.sem_inc(S["accd"], 4)
            dve.sem_inc(S["l2_add"], 4)
            dve.sem_inc(S["l2_acc"], 4)
            dve.sem_inc(S["sg_sel"], 3)
            for n in ("d_res", "p_split", "g_ag2", "g_xn", "f_res", "f_out"):
                dve.sem_inc(S[n], 2)

            dve.memset(src_i, -1).then_inc(S["pads_set"], 1)
            dve.memset(dst_i, -1).then_inc(S["pads_set"], 1)
            dve.memset(w_nat_e, 0.0).then_inc(S["pads_set"], 1)
            dve.memset(dst_next, 1 << 20).then_inc(S["pads_set"], 1)
            dve.memset(zeros[:, :], 0.0)
            dve.memset(x_sb[:, NB - 1:NBE, :], 0.0)
            dve.memset(pay[:, 0:J, 3:4], 0.0)
            dve.memset(pay[:, J:J + RING, :], 0.0)
            dve.wait_ge(S["consts"], 9)
            dve.tensor_copy(ident_b[:, :], ident[:, :])
            dve.tensor_copy(iota[:, :], iota_i[:, :])
            dve.tensor_copy(iota_b[:, :], iota_i[:, :])
            dve.tensor_copy(tile_no[:, :], tile_no_i[:, :])
            link(dve.tensor_scalar(node_real[:, :], node_i[:, :], float(N), None, ALU.is_lt))
            dve.wait_ge(S["edges_in"], 16 * 12)
            dve.tensor_copy(pay[:, 0:J, 0:1].rearrange("p j a -> p (j a)"), src_i[:, 0:J])
            dve.tensor_copy(pay[:, 0:J, 1:2].rearrange("p j a -> p (j a)"), dst_i[:, 0:J])
            dve.tensor_copy(pay[:, 0:J, 2:3].rearrange("p j a -> p (j a)"), w_nat_e)
            dve.tensor_tensor(pos_f, dst_i[:, 0:J], dst_next[:, 0:J], ALU.is_gt)
            link(dve.tensor_scalar(scan_out.bitcast(I32), src_i[:, 0:J], P - 1, None, ALU.bitwise_and))
            link(dve.tensor_copy(src_loc, scan_out.bitcast(I32)))
            dve.tensor_reduce(viol[:, :], pos_f, AX_X, ALU.add)
            link(dve.tensor_scalar(scan_out.bitcast(I32), src_i[:, 0:J], 7, None, ALU.arith_shift_right))
            dve.tensor_copy(src_blk, scan_out.bitcast(I32))
            link(dve.tensor_copy(src_kb, scan_out.bitcast(I32)))
            link(dve.tensor_scalar(scan_out.bitcast(I32), dst_i[:, 0:J], 7, None, ALU.arith_shift_right))
            link(dve.tensor_copy(dst_kb, scan_out.bitcast(I32)))
            with dve.Fori(0, NB) as b:
                chain.enter(b, 2)
                link(dve.tensor_scalar(pos_f, dst_kb, iota[:, ds(b, 1)], 0.0, ALU.is_equal, ALU.add, accum_out=sm["tot_d"][:, ds(b, 1)]))
                link(dve.tensor_scalar(scan_out, src_kb, iota[:, ds(b, 1)], 0.0, ALU.is_equal, ALU.add, accum_out=sm["tot_s"][:, ds(b, 1)]))
            chain.leave(NB)
            dve.sem_inc(S["totals_ready"], 1)
            dve.wait_ge(S["prefix_done"], 1)
            link(dve.tensor_copy(flag_i[:, :], bank[1][:, 128:129]))
            dve.sem_inc(S["flag_ready"], 1)

            def plan_tiles(k, base, win_i):
                c = {n: sm[n][:, 0:NB] for n in ("incl", "off", "t_a", "t_b", "t_incl", "delta", "ge")}
                ia, ib = sm_i["ti_a"][:, 0:NB], sm_i["ti_b"][:, 0:NB]
                total = bank[k][:, 64:64 + NB]
                link(dve.tensor_copy(c["t_a"], total))
                link(dve.tensor_tensor_scan(c["incl"], c["t_a"], c["t_a"], 0.0, ALU.add, ALU.bypass))
                link(dve.tensor_tensor(c["off"], c["incl"], c["t_a"], ALU.subtract))
                link(dve.scalar_tensor_tensor(base[:, 0:NB], c["off"], -1.0, bank[k][:, 0:NB], ALU.add, ALU.add))
                link(dve.tensor_copy(ia, c["off"]))
                link(dve.tensor_scalar(ib, ia, 4, None, ALU.arith_shift_right))
                link(dve.tensor_copy(c["t_b"], ib))
                link(dve.scalar_tensor_tensor(c["t_a"], c["t_b"], -float(CHUNK), c["incl"], ALU.mult, ALU.add))
                link(dve.tensor_scalar(c["t_a"], c["t_a"], float(P - 1), None, ALU.add))
                link(dve.tensor_copy(ia, c["t_a"]))
                link(dve.tensor_scalar(ib, ia, 7, None, ALU.arith_shift_right))
                link(dve.tensor_copy(c["t_a"], ib))
                link(dve.tensor_tensor_scan(c["t_incl"], c["t_a"], c["t_a"], 0.0, ALU.add, ALU.bypass))
                link(dve.tensor_tensor(c["t_a"], c["t_incl"], c["t_a"], ALU.subtract))
                link(dve.scalar_tensor_tensor(c["t_b"], c["t_a"], -float(P // CHUNK), c["t_b"], ALU.mult, ALU.add))
                link(dve.memset(sm["delta"][:, NB - 1:NB], float(2 * NROW)))
                link(dve.tensor_tensor(sm["delta"][:, 0:NB - 1], sm["t_b"][:, 1:NB], sm["t_b"][:, 0:NB - 1], ALU.subtract))
                for g in range(TG):
                    t = tile_no[:, g:g + 1]
                    link(dve.tensor_scalar(c["ge"], c["t_incl"], t, None, ALU.is_le))
                    link(dve.tensor_reduce(ge_sum[:, g:g + 1], c["ge"], AX_X, ALU.add))
                    link(dve.tensor_tensor(c["ge"], c["ge"], c["delta"], ALU.mult))
                    link(dve.tensor_reduce(row_b[:, g:g + 1], c["ge"], AX_X, ALU.add))
                link(dve.tensor_scalar(blk_c[:, :], ge_sum[:, :], float(NB - 1), None, ALU.min))
                link(dve.tensor_scalar(row_b[:, :], row_b[:, :], sm["t_b"][:, 0:1], None, ALU.add))
                link(dve.scalar_tensor_tensor(row_b[:, :], tile_no[:, :], float(P // CHUNK), row_b[:, :], ALU.mult, ALU.add))
                for g in range(TG):
                    link(dve.tensor_scalar(win_i[:, g, :], iota[:, 0:P // CHUNK], row_b[:, g:g + 1], float(NROW - 1), ALU.add, ALU.min))

            def place_blocks(k, blk):
                for g in range(TG):
                    if g >= 2 or k:
                        dve.wait_ge(S["blk_bcast"], k * TG + g - 1)
                    dve.tensor_scalar(diag[:, g % 2, :], ident[:, :], blk_c[:, g:g + 1], None, ALU.mult).then_inc(S["diag_ready"], 1)
                dve.wait_ge(S["blk_bcast"], (k + 1) * TG)
                dve.tensor_copy(blk[:, 0:512], bank[2][:, :])
                link(dve.tensor_copy(blk[:, 512:TC], bank[3][:, 0:TC - 512]))

            plan_tiles(0, sm["base_d"], win_i_d)
            dve.sem_inc(S["win_d_ready"], 1)
            for g in range(TG):
                link(dve.tensor_scalar(tile_oh[:, g, :], iota[:, 0:NB], blk_c[:, g:g + 1], None, ALU.is_equal))
            place_blocks(0, blk_d)
            plan_tiles(1, sm["base_s"], win_i_s)
            dve.sem_inc(S["win_s_ready"], 1)
            place_blocks(1, blk_s)

            def positions(kb, base, pos):
                link(dve.tensor_copy(pos_f, pos_start[:, :]))
                with dve.Fori(0, NB) as b:
                    chain.enter(b, 3)
                    link(dve.tensor_scalar(mask, kb, iota[:, ds(b, 1)], None, ALU.is_equal))
                    link(dve.tensor_tensor_scan(scan_out, mask, mask, base[:, ds(b, 1)], ALU.add, ALU.bypass))
                    apart(dve, S["waited"])
                    link(dve.copy_predicated(pos_f, mask.bitcast(I16), scan_out))
                chain.leave(NB)
                link(dve.tensor_copy(pos[:, 0:J], pos_f))

            link(dve.memset(pos_s[:, J:J + RING], 0))
            positions(src_kb, sm["base_s"], pos_s)
            dve.sem_inc(S["pos_s_ready"], 1)
            unsorted = dve.value_load(flag_i[0:1, 0:1], min_val=0, max_val=E)
            with dve.If(unsorted > 0):
                positions(dst_kb, sm["base_d"], pos_d)
                dve.sem_inc(S["slow_pos"], 1)
            with dve.Else():
                dve.sem_inc(S["dve_chain"], 3 * NB + 2)

            dve.wait_ge(S["wt_copied"], len(TURN) + 6)
            link(dve.tensor_copy(val_a[:, :], blk_d[:, :]))
            link(dve.scalar_tensor_tensor(d_loc[:, :], val_a, -float(P), d_loc[:, :], ALU.mult, ALU.add))
            link(dve.tensor_copy(val_b.bitcast(I32), d_idx[:, :]))
            link(dve.tensor_scalar(val_a.bitcast(I32), val_b.bitcast(I32), P - 1, None, ALU.bitwise_and))
            link(dve.tensor_copy(d_sloc, val_a.bitcast(I32)))
            link(dve.tensor_scalar(val_a.bitcast(I32), val_b.bitcast(I32), 7, None, ALU.arith_shift_right))
            link(dve.tensor_copy(d_sblk, val_a.bitcast(I32)))
            link(dve.tensor_scalar(d_idx[:, :], d_idx[:, :], 0.0, None, ALU.max))

            def split3(dst, src, rest):
                link(dve.tensor_copy(dst(0), src))
                link(dve.tensor_tensor(rest, src, dst(0), ALU.subtract))
                link(dve.tensor_copy(dst(1), rest))
                link(dve.tensor_tensor(dst(2), rest, dst(1), ALU.subtract))

            part_of = lambda s: parts[:, :, s:s + 1].rearrange("p t a -> p (t a)")
            link(dve.memset(part_of(3), 1.0))

            def segment_onehots(k):
                dve.sem_inc(S["seg_ready"], 1)
                with dve.Fori(0, TURNS) as i:
                    for g in range(GROUPS):
                        dve.wait_ge(S["seg_mm"], i * GROUPS + T // GROUP * k + g + 1)
                        for u in range(GROUP):
                            o = dve.tensor_scalar(ohb[:, g % 3 * GROUP + u, :], iota_b[:, :], d_loc[:, ds(i * SPAN + 4 * g + u, 1)],
                                                  None, ALU.is_equal)
                        o.then_inc(S["seg_oh"], 1)
                dve.wait_ge(S["seg_cp"], T // 4 * (k + 1) + 2)

            def combine(k, first, last, dst):
                w = lambda s: tile_sums[:, 0:T, s:s + 1].rearrange("p t a -> p (t a)")
                link(dve.tensor_copy(val_b[:, 0:T], w(first)))
                for s in range(first + 1, last + 1):
                    link(dve.tensor_tensor(val_b[:, 0:T], val_b[:, 0:T], w(s), ALU.add))
                link(dve.memset(val_b[:, T:TC], 0.0))
                dve.sem_inc(S["comb_v"], 1)
                dve.wait_ge(S["comb_done"], k + 1)
                link(dve.tensor_copy(dst[:, 0:NB], bank[1][:, 0:NB]))

            def node_values(k, values, loc, blk, to):
                split3(lambda s: table3[:, s, 0:NB], values[:, 0:NB], sm["t_b"][:, 0:NB])
                dve.sem_inc(S["sg_ready"], 1)

                def turn_of(i, first, last):
                    for g in range(3 if last else GROUPS):
                        m = i * GROUPS + T // GROUP * k + g
                        if not last:
                            dve.wait_ge(S["sg_t"], m + 1)
                            for u in range(GROUP):
                                o = dve.tensor_scalar(ohb[:, g % 3 * GROUP + u, :], iota_b[:, :], loc[:, ds(i * SPAN + 4 * g + u, 1)],
                                                      None, ALU.is_equal)
                            o.then_inc(S["sg_oh"], 1)
                        if runs(g, 3, first, last):
                            dve.wait_ge(S["sg_mm"], m - 3 + 1 + 3)
                            dve.wait_ge(S["sg_sel"], m - 3 + 3)
                            for u in range(GROUP):
                                t = ds(i * SPAN + 4 * (g - 3) + u, 1)
                                sel = dve.scalar_tensor_tensor(junk[:, u, 0:NB], iota[:, 0:NB], blk[:, t],
                                                               bank[SG_S[g % 3]][:, u * 64:u * 64 + NB],
                                                               ALU.is_equal, ALU.mult, accum_out=to[:, t])
                            sel.then_inc(S["sg_sel"], 1)

                in_turns(dve, TURNS, turn_of, 3)
                dve.wait_ge(S["sg_sel"], T // GROUP * (k + 1) + 3)

            split3(part_of, d_norm[:, :], val_a)
            segment_onehots(0)
            combine(0, 0, 2, sm["deg_in"])
            combine(1, 3, 3, sm["cnt_in"])
            with dve.Fori(0, J // SPAN) as i:
                for g in range(GROUPS):
                    dve.wait_ge(S["deg_mm"], i * GROUPS + g + 1)
                    for u in range(GROUP):
                        v, t = g % 2 * GROUP + u, ds(i * SPAN + 4 * g + u, 1)
                        dve.tensor_scalar(oh[:, 4 + v, :], iota[:, :], src_loc[:, t], w_nat_e[:, t], ALU.is_equal, ALU.mult)
                        o = dve.tensor_scalar(junk[:, v, 0:NB], iota[:, 0:NB], src_blk[:, t], None, ALU.is_equal)
                    o.then_inc(S["deg_oh"], 1)
            dve.wait_ge(S["deg_mm"], J // GROUP + 2)
            link(dve.tensor_copy(sm["deg_out"][:, 0:NB], bank[0][:, 0:NB]))
            link(dve.tensor_copy(s_idx[:, :], blk_d[:, :]))
            node_values(0, sm["deg_in"], d_loc, s_idx, val_b)
            node_values(1, sm["deg_out"], d_sloc, d_sblk, val_a)
            link(dve.tensor_tensor(val_a[:, 0:T], val_a[:, 0:T], val_b[:, 0:T], ALU.mult))
            link(dve.tensor_scalar(val_a[:, 0:T], val_a[:, 0:T], 1e-12, None, ALU.add))
            dve.sem_inc(S["sqrt_in"], 1)
            dve.wait_ge(S["sqrt_out"], 1)
            link(dve.reciprocal(val_a[:, 0:T], val_a[:, 0:T]))
            link(dve.tensor_tensor(d_norm[:, 0:T], d_norm[:, 0:T], val_a[:, 0:T], ALU.mult))
            dve.sem_inc(S["l0_ready"], 1)
            dve.wait_ge(S["wt_copied"], len(TURN) + 10)
            link(dve.tensor_copy(val_a[:, :], blk_s[:, :]))
            link(dve.scalar_tensor_tensor(s_loc[:, :], val_a, -float(P), s_loc[:, :], ALU.mult, ALU.add))
            link(dve.tensor_scalar(s_idx[:, :], s_idx[:, :], 0.0, None, ALU.max))

            def scatter_pass(k, loc, weight, blk, lo, width):
                with dve.Fori(0, TURNS) as i:
                    def add(u):
                        if u % RING == 0:
                            dve.load(regs, blk[0:1, ds(i * SPAN + u, RING)])
                        n = i * SPAN + T * k + u
                        b = dve.snap(regs[u % RING], min_val=0, max_val=NB - 1)
                        dve.wait_ge(S["mm"], n + 1 + 8)
                        dve.wait_ge(S["accd"], n + 4)
                        to = acc[:, ds(b, 1), lo:lo + width].rearrange("p a f -> p (a f)")
                        dve.tensor_tensor(to, bank[u % 4][:, 0:width], to, ALU.add).then_inc(S["accd"], 1)

                    for u in range(SPAN + 2):
                        if u < SPAN:
                            t = ds(i * SPAN + u, 1)
                            dve.wait_ge(S["mm"], i * SPAN + T * k + u + 5)
                            if weight is None:
                                o = dve.tensor_scalar(oh[:, u % 4, :], iota[:, :], loc[:, t], None, ALU.is_equal)
                            else:
                                o = dve.tensor_scalar(oh[:, u % 4, :], iota[:, :], loc[:, t], weight[:, t], ALU.is_equal, ALU.mult)
                            o.then_inc(S["one_hot"], 1)
                        if u >= 2:
                            add(u - 2)
                dve.wait_ge(S["accd"], T * (k + 1) + 4)

            def stage_block(n, q, base):
                dve.wait_ge(S["d_t"], n + base + 1)
                dve.tensor_scalar(staged_x[:, q, :], acc[:, ds(n, 1), 0:D].rearrange("p a f -> p (a f)"), 1.0, None, ALU.mult).then_inc(S["d_staged"], 1)

            x_of = lambda n: x_sb[:, ds(n, 1), :].rearrange("p a f -> p (a f)")

            def statistics(n, q):
                apart(dve, S["waited"])
                link(dve.bn_stats(stats[:, q, :], x_of(n)))
                apart(dve, S["waited"])
                link(dve.bn_aggr(mv_one[:, q, :], stats[:, q, :]))
                return dve.tensor_scalar(mv[:, ds(n, 1), :].rearrange("p a w -> p (a w)"), mv_one[:, q, :], 1.0, None, ALU.mult)

            def pair_statistics(i):
                apart(dve, S["waited"])
                for q in range(2):
                    o = dve.bn_stats(stats[:, q, :], x_of(i * 2 + q))
                link(o)
                apart(dve, S["waited"])
                for q in range(2):
                    o = dve.bn_aggr(mv_one[:, q, :], stats[:, q, :])
                link(o)
                link(dve.tensor_scalar(mv[:, ds(i * 2, 2), :].rearrange("p b w -> p (b w)"), mv_one[:, :, :].rearrange("p b w -> p (b w)"),
                                       1.0, None, ALU.mult))

            pair_of = lambda i: x_sb[:, ds(i * 2, 2), :]
            on_both = lambda row: row.unsqueeze(1).to_broadcast([P, 2, D])
            sqrts = [1]

            def square_root(x):
                sqrts[0] += 1
                dve.sem_inc(S["sqrt_in"], 1)
                dve.wait_ge(S["sqrt_out"], sqrts[0])
                link(dve.reciprocal(x, x))

            mean, rstd = sm["mean"][:, 0:NBE], sm["rstd"][:, 0:NBE]

            def normalizers(masked=False):
                link(dve.tensor_copy(mean, mv[:, :, 0:1].rearrange("p b a -> p (b a)")))
                link(dve.tensor_scalar(rstd, mv[:, :, 1:2].rearrange("p b a -> p (b a)"), 1e-5, None, ALU.add))
                square_root(rstd)
                if masked:
                    link(dve.tensor_tensor(rstd, rstd, node_real[:, :], ALU.mult))

            def normalize(to, n):
                return dve.tensor_scalar(to, x_of(n), mean[:, ds(n, 1)], rstd[:, ds(n, 1)], ALU.subtract, ALU.mult)

            dve.wait_ge(S["wt_stored"], 32)
            link(dve.memset(acc_flat, 0.0))
            scatter_pass(0, d_loc, d_norm, blk_d, 0, D)
            with dve.Fori(0, PAIRS) as i:
                for q in range(2):
                    stage_block(i * 2 + q, q, 0)
            dve.wait_ge(S["d_staged"], NBE)
            link(dve.memset(acc_flat, 0.0))
            scatter_pass(1, d_loc, d_norm, blk_d, 0, D)
            dve.wait_ge(S["x_in"], 32)
            with dve.Fori(0, PAIRS) as i:
                chain.enter(i, 6)
                for q in range(2):
                    stage_block(i * 2 + q, q, NBE)
                for q in range(2):
                    n = i * 2 + q
                    dve.wait_ge(S["d_m2"], n + 1 + 2)
                    link(dve.tensor_tensor(x_of(n), bank[2 + q][:, 0:D], x_of(n), ALU.add))
                    statistics(n, q).then_inc(S["d_res"], 1)
            chain.leave(PAIRS)
            dve.wait_ge(S["d_res"], NBE + 2)
            normalizers(masked=True)
            link(dve.memset(sm["t_a"][:, 0:NBE], 0.0))
            link(dve.tensor_scalar(sm["t_a"][:, 0:NB], sm["cnt_in"][:, 0:NB], 0.0, None, ALU.add))
            link(dve.tensor_scalar(sm["t_a"][:, 0:NBE], sm["t_a"][:, 0:NBE], 1.0, None, ALU.add))
            square_root(sm["t_a"][:, 0:NBE])
            link(dve.tensor_copy(sm["dis"][:, 0:NBE], sm["t_a"][:, 0:NBE]))
            with dve.Fori(0, PAIRS) as i:
                chain.enter(i, 2)
                normalize(x_of(i * 2), i * 2)
                link(normalize(x_of(i * 2 + 1), i * 2 + 1))
                dve.sem_inc(S["col_ready"], 2)
                for q in range(2):
                    o = dve.scalar_tensor_tensor(tmp_q[:, q, :], x_of(i * 2 + q), 1.0, gw_bc[:, :], ALU.mult, ALU.mult,
                                                 accum_out=sm["h"][:, ds(i * 2 + q, 1)])
                link(o)
            chain.leave(PAIRS)
            dve.wait_ge(S["col_done"], NBE)
            link(dve.tensor_scalar(staged_x[0:1, 0, :], bank[0][0:1, 256:256 + D], 1.0 / N, None, ALU.mult))
            dve.sem_inc(S["gate_step"], 1)
            dve.wait_ge(S["pe_chain"], 4)
            link(dve.tensor_scalar(gate_bc[:, :], bank[4][:, 0:D], 2.0, None, ALU.add))
            dve.sem_inc(S["gate_done"], 1)
            link(dve.tensor_tensor(sm["hd"][:, 0:NB], sm["h"][:, 0:NB], sm["dis"][:, 0:NB], ALU.mult))
            node_values(2, sm["hd"], d_sloc, d_sblk, val_a)
            link(dve.memset(val_a[:, T:TC], 0.0))
            split3(part_of, val_a, val_b)
            segment_onehots(1)
            combine(2, 0, 2, sm["spa"])
            link(dve.tensor_tensor(sm["spa"][:, 0:NB], sm["spa"][:, 0:NB], sm["hd"][:, 0:NB], ALU.add))
            link(dve.tensor_tensor(sm["spa"][:, 0:NB], sm["spa"][:, 0:NB], sm["dis"][:, 0:NB], ALU.mult))
            link(dve.memset(sm["spa"][:, NB:NBE], 0.0))
            dve.sem_inc(S["spa_in"], 1)
            dve.wait_ge(S["spa_out"], 1)
            with dve.Fori(0, PAIRS) as i:
                chain.enter(i, 4)
                for q in range(2):
                    n = i * 2 + q
                    o = dve.scalar_tensor_tensor(x_of(n), gate_bc[:, :], sm["spa"][:, ds(n, 1)], x_of(n), ALU.add, ALU.mult)
                link(o)
                pair_statistics(i)
            chain.leave(PAIRS)
            normalizers()
            with dve.Fori(0, NBE) as b:
                normalize(x_of(b), b).then_inc(S["x2_done"], 1)
            dve.wait_ge(S["p_loaded"], 16)
            link(dve.memset(acc_flat, 0.0))
            with dve.Fori(0, PAIRS) as i:
                chain.enter(i, 6)
                for q in range(2):
                    n = i * 2 + q
                    dve.wait_ge(S["d_m"], n + 2 * NBE + 1 + 2)
                    s3 = lambda s: p3[:, s, ds(n, 1), :].rearrange("p a f -> p (a f)")
                    P_b = bank[6 + q][:, 0:D]
                    link(dve.tensor_copy(s3(0), P_b))
                    link(dve.tensor_tensor(tmp_q[:, q, :], P_b, s3(0), ALU.subtract))
                    link(dve.tensor_copy(s3(1), tmp_q[:, q, :]))
                    dve.tensor_tensor(s3(2), tmp_q[:, q, :], s3(1), ALU.subtract).then_inc(S["p_split"], 1)
            chain.leave(PAIRS)
            dve.wait_ge(S["p_split"], NBE + 2)
            link(dve.memset(msg[:, :, D:D + 1], 1.0))
            dve.sem_inc(S["pass_ready"], 1)

            def l2_sums(i, first, last):
                for g in range(3 if last else GROUPS):
                    if not last:
                        dve.wait_ge(S["l2_c"], i * SPAN + 4 * g + 4)
                        for u in range(GROUP):
                            t = 4 * g + u
                            dve.tensor_scalar(oh[:, t % 12, :], iota[:, :], s_loc[:, ds(i * SPAN + t, 1)], None, ALU.is_equal).then_inc(S["l2_oh"], 1)
                    if runs(g, 3, first, last):
                        for u in range(GROUP):
                            t = 4 * (g - 3) + u
                            if t % RING == 0:
                                dve.load(regs, blk_s[0:1, ds(i * SPAN + t, RING)])
                            b = dve.snap(regs[t % RING], min_val=0, max_val=NB - 1)
                            dve.wait_ge(S["l2_c"], i * SPAN + t + 1 + 12)
                            dve.wait_ge(S["l2_acc"], i * SPAN + t + 4)
                            to = acc[:, ds(b, 1), :].rearrange("p a f -> p (a f)")
                            dve.tensor_tensor(to, bank[4 + u][:, 0:D + 1], to, ALU.add).then_inc(S["l2_acc"], 1)
                    if runs(g, 1, first, last):
                        for t in range(4 * (g - 1), 4 * g, 2):
                            dve.wait_ge(S["l2_p"], i * (SPAN // 2) + t // 2 + 1 + 4)
                            for w in range(t, t + 2):
                                dve.wait_ge(gd[w % RING], i * 48 + 16 * (T // RING * 2 + w // RING + 1))
                            dve.wait_ge(S["l2_c"], i * SPAN + t + 6)
                            both = slice(t % RING, t % RING + 2)
                            dve.tensor_tensor(msg[:, both, 0:D], bank[2 + t // 2 % 2][:, :].rearrange("p (r f) -> p r f", r=2),
                                              gbuf[:, both, 0:D], ALU.add).then_inc(S["l2_add"], 1)

            in_turns(dve, TURNS, l2_sums, 3)
            dve.wait_ge(S["l2_acc"], T + 4)
            dve.sem_inc(S["g_done"], 1)
            dve.wait_ge(S["w5_in"], 16 * 9)
            link(dve.memset(ones_b[:, :], 1.0))
            for c in range(0, 6 * D, 2 * D):
                b, to = gru_bias[:, c:c + 2 * D], gru_rows[:, c:c + 2 * D]
                link(dve.tensor_copy(part_rows, b))
                link(dve.tensor_tensor(rest_rows, b, part_rows, ALU.subtract))
                link(dve.tensor_scalar(to, part_rows, ident[0:3, 0:1], None, ALU.mult))
                link(dve.tensor_copy(part_rows, rest_rows))
                link(dve.tensor_tensor(rest_rows, rest_rows, part_rows, ALU.subtract))
                link(dve.scalar_tensor_tensor(to, part_rows, ident[0:3, 1:2], to, ALU.mult, ALU.add))
                link(dve.scalar_tensor_tensor(to, rest_rows, ident[0:3, 2:3], to, ALU.mult, ALU.add))
            dve.sem_inc(S["gru_rows"], 1)

            def mean_messages(i):
                for q in range(2):
                    n = i * 2 + q
                    cnt = acc[:, ds(n, 1), D:D + 1].rearrange("p a f -> p (a f)")
                    dve.wait_ge(S["g_t1"], n + 1)
                    link(dve.tensor_scalar(cnt_c[:, q, 0:1], cnt, 1e-8, None, ALU.add))
                    link(dve.reciprocal(cnt_c[:, q, 0:1], cnt_c[:, q, 0:1]))
                    link(dve.tensor_tensor(cnt_c[:, q, 1:2], cnt, cnt_c[:, q, 0:1], ALU.mult))
                    dve.tensor_scalar(staged_x[:, q, :], acc[:, ds(n, 1), 0:D].rearrange("p a f -> p (a f)"), cnt_c[:, q, 0:1],
                                      None, ALU.mult).then_inc(S["g_agg"], 1)

            def aggregates(i):
                for q in range(2):
                    n = i * 2 + q
                    dve.wait_ge(S["g_m"], n + 1 + 2)
                    dve.wait_ge(S["g_t2"], n + 1)
                    dve.tensor_scalar(hq[:, q, :], x_of(n), 1.0, None, ALU.mult)
                    dve.scalar_tensor_tensor(tmp_q[:, q, :], b2_bc, cnt_c[:, q, 1:2], bank[q][:, D:2 * D],
                                             ALU.mult, ALU.add).then_inc(S["g_ag2"], 1)

            def new_state(n, q):
                dve.wait_ge(S["g_rz"], n + 1)
                link(dve.tensor_tensor(n_sb[:, q, :], bank[4 + 2 * q][:, D:2 * D], rz[:, q, 0:D], ALU.mult))
                dve.tensor_tensor(n_sb[:, q, :], bank[4 + 2 * q][:, 0:D], n_sb[:, q, :], ALU.add).then_inc(S["g_n"], 1)
                dve.wait_ge(S["g_tanh"], n + 1 + 2)
                link(dve.tensor_tensor(rz[:, q, 0:D], x_of(n), n_sb[:, q, :], ALU.subtract))
                link(dve.tensor_tensor(rz[:, q, 0:D], rz[:, q, 0:D], rz[:, q, D:2 * D], ALU.mult))
                link(dve.tensor_tensor(x_of(n), rz[:, q, 0:D], n_sb[:, q, :], ALU.add))
                statistics(n, q).then_inc(S["g_xn"], 1)

            mean_messages(0)
            dve.wait_ge(S["x2_first"], 16)
            aggregates(0)
            mean_messages(1)
            dve.wait_ge(S["x2_rest"], 16)
            with dve.Fori(1, PAIRS - 1) as i:
                chain.enter(i - 1, 18)
                new_state(i * 2 - 2, 0)
                aggregates(i)
                mean_messages(i + 1)
                new_state(i * 2 - 1, 1)
            chain.leave(PAIRS - 2)
            new_state(NBE - 4, 0)
            aggregates(PAIRS - 1)
            new_state(NBE - 3, 1)
            new_state(NBE - 2, 0)
            new_state(NBE - 1, 1)
            dve.wait_ge(S["g_xn"], NBE + 2)
            normalizers()
            with dve.Fori(0, PAIRS) as i:
                chain.enter(i, 6)
                for q in range(2):
                    dve.wait_ge(pair["x2b_in"][q], i * 16 + 16)
                dve.tensor_tensor(hq[:, :, :], hq[:, :, :], on_both(beta_bc), ALU.add)
                normalize(x_of(i * 2), i * 2)
                link(normalize(x_of(i * 2 + 1), i * 2 + 1))
                link(dve.tensor_tensor(pair_of(i), pair_of(i), on_both(gamma_bc), ALU.mult))
                link(dve.tensor_tensor(pair_of(i), pair_of(i), hq[:, :, :], ALU.add))
                dve.sem_inc(S["f_res"], 2)
                pair_statistics(i)
            chain.leave(PAIRS)
            dve.wait_ge(S["f_res"], NBE + 2)
            normalizers()
            link(dve.tensor_scalar(sm["t_a"][:, 0:NBE], acc[:, :, D:D + 1].rearrange("p b a -> p (b a)"), 1.0, None, ALU.add))
            square_root(sm["t_a"][:, 0:NBE])
            link(dve.tensor_copy(sm["ri"][:, 0:NBE], sm["t_a"][:, 0:NBE]))
            link(dve.memset(acc_flat, 0.0))
            scales = (sm["dis"], sm["ri"])

            def d6(i, first, last):
                if not last:
                    for q in range(2):
                        n = i * 2 + q
                        dve.wait_ge(S["d_t"], n + 3 * NBE + 1)
                        normalize(staged_x[:, q, :], n).then_inc(S["d_staged"], 1)
                    dve.wait_ge(S["d_staged"], i * 2 + 2 + 2 * NBE)
                    for q in range(2):
                        o = normalize(x_of(i * 2 + q), i * 2 + q)
                    o.then_inc(S["x3_done"], 1)
                if first:
                    return
                for q in range(2):
                    n = i * 2 - 2 + q
                    dve.wait_ge(S["d_m"], n + 3 * NBE + 1 + 2)
                    dve.wait_ge(pair["tab_out"][q], i * 32 - 32 + 16 * PAIRS)
                    dve.tensor_scalar(hq[:, q, 0:P], bank[6 + q][:, 0:P], scales[0][:, ds(n, 1)], None, ALU.mult)
                    dve.tensor_scalar(hq[:, q, P:D], bank[6 + q][:, P:D], scales[1][:, ds(n, 1)], None, ALU.mult).then_inc(S["d_h"], 1)

            in_turns(dve, PAIRS, d6, 1)
            dve.wait_ge(S["x3_done"], PAIRS)
            scatter_pass(2, s_loc, None, blk_s, 0, P)
            scatter_pass(3, d_loc, None, blk_d, P, P)
            dve.sem_inc(S["final_ready"], 1)
            with dve.Fori(0, PAIRS) as i:
                chain.enter(i, 6)
                for q in range(2):
                    dve.wait_ge(pair["fin_in"][q], i * 32 + 32)
                link(dve.tensor_tensor(tmp_q, acc[:, ds(i * 2, 2), 0:D], hq[:, :, :], ALU.add))
                dve.sem_inc(S["f_out"], 2)
                for q in range(2):
                    n = i * 2 + q
                    dve.scalar_tensor_tensor(tmp_q[:, q, 0:P], tmp_q[:, q, 0:P], sm["ri"][:, ds(n, 1)], bias_bc[:, 0:P], ALU.mult, ALU.add)
                    o = dve.scalar_tensor_tensor(tmp_q[:, q, P:D], tmp_q[:, q, P:D], sm["dis"][:, ds(n, 1)], bias_bc[:, P:D], ALU.mult, ALU.add)
                link(o)
                link(dve.tensor_tensor(pair_of(i), pair_of(i), tmp_q, ALU.add))
                pair_statistics(i)
            chain.leave(PAIRS)
            normalizers()

            def last_norm(i, first):
                for q in range(2):
                    if not first:
                        dve.wait_ge(pair["y_out"][q], i * 16)
                    normalize(staged_x[:, q, :], i * 2 + q).then_inc(S["y_ready"], 1)

            last_norm(0, True)
            with dve.Fori(1, PAIRS) as i:
                last_norm(i, False)


INPUTS = ["x", "src", "dst", "edge_weight", "L0_gnn_W6", "L0_gnn_b6", "L0_gnn_W7", "L0_gnn_b7", "L0_gnn_Wp", "L0_gnn_bp",
          "L1_gnn_w1", "L1_gnn_b1", "L1_gnn_w2", "L1_gnn_b2", "L1_gnn_gcn_w", "L1_gnn_gcn_b", "L2_gnn_W1", "L2_gnn_b1",
          "L2_gnn_W2", "L2_gnn_b2", "L2_gnn_w_ih", "L2_gnn_w_hh", "L2_gnn_b_ih", "L2_gnn_b_hh", "L2_gnn_gamma", "L2_gnn_beta",
          "L3_gnn_W_f", "L3_gnn_W_b", "L3_gnn_bias_param"]


def kernel(**inputs):
    import numpy as np
    import concourse.bacc as bacc
    from concourse.bass_utils import run_bass_kernel_spmd

    nc = bacc.Bacc("TRN2", target_bir_lowering=False, num_devices=1)
    arrays, aps = {}, {}
    for name in INPUTS:
        a = np.ascontiguousarray(inputs[name])
        arrays[f"in_{name}"] = a
        aps[name] = nc.dram_tensor(f"in_{name}", a.shape, mybir.dt.from_np(a.dtype), kind="ExternalInput").ap()
    out = nc.dram_tensor("out_0", inputs["x"].shape, F32, kind="ExternalOutput").ap()
    build(nc, aps, out)
    return run_bass_kernel_spmd(nc, [arrays], core_ids=[0]).results[0]["out_0"]
```
